# Optimizing a Trainium2 kernel written in Bass

```python
import numpy as np
import jax
import jax.numpy as jnp

def _softmax(x, axis=-1):
    return jax.nn.softmax(x, axis=axis)

def _gelu(x):
    return jax.nn.gelu(x, approximate=True)

def _silu(x):
    return jax.nn.silu(x)

def _sigmoid(x):
    return jax.nn.sigmoid(x)

def _layernorm(x, axis=-1, eps=1e-05):
    m = jnp.mean(x, axis=axis, keepdims=True)
    v = jnp.var(x, axis=axis, keepdims=True)
    return (x - m) / jnp.sqrt(v + eps)

def _scatter_add(tgt, idx, src, axis=0):
    return tgt.at[idx].add(src)

def _segment_sum(src, seg, n):
    return jax.ops.segment_sum(src, seg, n)
kernel_name = 'mk_seq_preln_d1_jaxref_r8_7bbbba'

def setup_inputs(seed: int=0):
    np.random.seed(seed)
    _w = jnp.asarray

    def _L0_attn_setup():
        import jax, jax.numpy as jnp
        import numpy as np
        EMBED_DIM = 128
        NUM_HEADS = 16
        HEAD_DIM = EMBED_DIM // NUM_HEADS
        LORA_R = 8
        ALPHA = 1.0
        B, S = (2, 256)

        def lora_linear(x, W, b, A, Bm):
            return x @ W.T + b + x @ A.T @ Bm.T * (ALPHA / LORA_R)
        key = jax.random.key(seed)
        ks = jax.random.split(key, 20)
        d = {'x': jax.random.normal(ks[0], (B, S, EMBED_DIM), dtype=jnp.float32)}
        names = ['q', 'k', 'v', 'o']
        i = 1
        for n in names:
            d['W' + n] = jax.random.normal(ks[i], (EMBED_DIM, EMBED_DIM), jnp.float32) * 0.02
            i += 1
            d['b' + n] = jnp.zeros((EMBED_DIM,), jnp.float32)
            d['A' + n] = jax.random.normal(ks[i], (LORA_R, EMBED_DIM), jnp.float32) * 0.02
            i += 1
            d['B' + n] = jax.random.normal(ks[i], (EMBED_DIM, LORA_R), jnp.float32) * 0.02
            i += 1
        d['rezero'] = jnp.zeros((1,), jnp.float32) + 0.1
        return d
    _L0_attn_in = _L0_attn_setup()

    def _L0_ffn_setup():
        import jax, jax.numpy as jnp
        import numpy as np
        B, T, C = (4, 256, 128)
        E, H, K = (8, 256, 2)
        key = jax.random.key(seed)
        ks = jax.random.split(key, 7)
        s_in = 1.0 / np.sqrt(C)
        s_hid = 1.0 / np.sqrt(H)
        return {'x': jax.random.normal(ks[0], (B, T, C), dtype=jnp.float32), 'gate_w': jax.random.uniform(ks[1], (C, E), jnp.float32, -s_in, s_in), 'gate_b': jnp.zeros((E,), jnp.float32), 'w1': jax.random.uniform(ks[2], (E, C, H), jnp.float32, -s_in, s_in), 'b1': jax.random.uniform(ks[3], (E, H), jnp.float32, -s_in, s_in), 'w2': jax.random.uniform(ks[4], (E, H, C), jnp.float32, -s_hid, s_hid), 'b2': jax.random.uniform(ks[5], (E, C), jnp.float32, -s_hid, s_hid)}
    _L0_ffn_in = _L0_ffn_setup()
    _d = {'L0_attn_x': _L0_attn_in['x'], 'L0_attn_Wq': _L0_attn_in['Wq'], 'L0_attn_bq': _L0_attn_in['bq'], 'L0_attn_Aq': _L0_attn_in['Aq'], 'L0_attn_Bq': _L0_attn_in['Bq'], 'L0_attn_Wk': _L0_attn_in['Wk'], 'L0_attn_bk': _L0_attn_in['bk'], 'L0_attn_Ak': _L0_attn_in['Ak'], 'L0_attn_Bk': _L0_attn_in['Bk'], 'L0_attn_Wv': _L0_attn_in['Wv'], 'L0_attn_bv': _L0_attn_in['bv'], 'L0_attn_Av': _L0_attn_in['Av'], 'L0_attn_Bv': _L0_attn_in['Bv'], 'L0_attn_Wo': _L0_attn_in['Wo'], 'L0_attn_bo': _L0_attn_in['bo'], 'L0_attn_Ao': _L0_attn_in['Ao'], 'L0_attn_Bo': _L0_attn_in['Bo'], 'L0_attn_rezero': _L0_attn_in['rezero'], 'L0_ffn_gate_w': _L0_ffn_in['gate_w'], 'L0_ffn_gate_b': _L0_ffn_in['gate_b'], 'L0_ffn_w1': _L0_ffn_in['w1'], 'L0_ffn_b1': _L0_ffn_in['b1'], 'L0_ffn_w2': _L0_ffn_in['w2'], 'L0_ffn_b2': _L0_ffn_in['b2']}
    _x0 = _d['L0_attn_x']
    _d['L0_attn_x'] = jax.random.normal(jax.random.fold_in(jax.random.key(seed), 1), (16, 512, 128), dtype=_x0.dtype)
    del _x0
    return _d

def reference(L0_attn_x, L0_attn_Wq, L0_attn_bq, L0_attn_Aq, L0_attn_Bq, L0_attn_Wk, L0_attn_bk, L0_attn_Ak, L0_attn_Bk, L0_attn_Wv, L0_attn_bv, L0_attn_Av, L0_attn_Bv, L0_attn_Wo, L0_attn_bo, L0_attn_Ao, L0_attn_Bo, L0_attn_rezero, L0_ffn_gate_w, L0_ffn_gate_b, L0_ffn_w1, L0_ffn_b1, L0_ffn_w2, L0_ffn_b2):

    def _L0_attn_ref(x, Wq, bq, Aq, Bq, Wk, bk, Ak, Bk, Wv, bv, Av, Bv, Wo, bo, Ao, Bo, rezero):
        import jax, jax.numpy as jnp
        import numpy as np
        EMBED_DIM = 128
        NUM_HEADS = 16
        HEAD_DIM = EMBED_DIM // NUM_HEADS
        LORA_R = 8
        ALPHA = 1.0
        B, S = (2, 256)

        def lora_linear(x, W, b, A, Bm):
            return x @ W.T + b + x @ A.T @ Bm.T * (ALPHA / LORA_R)
        bsz, seq_len, _ = x.shape
        Q = lora_linear(x, Wq, bq, Aq, Bq).reshape(bsz, seq_len, NUM_HEADS, HEAD_DIM)
        K = lora_linear(x, Wk, bk, Ak, Bk).reshape(bsz, seq_len, NUM_HEADS, HEAD_DIM)
        V = lora_linear(x, Wv, bv, Av, Bv).reshape(bsz, seq_len, NUM_HEADS, HEAD_DIM)
        scores = jnp.einsum('bqhd,bkhd->bhqk', Q, K) / np.sqrt(HEAD_DIM).astype(np.float32)
        slopes = 0.5 ** jnp.arange(NUM_HEADS, dtype=jnp.float32)
        pos = jnp.arange(seq_len, dtype=jnp.float32)
        rel = pos[None, :] - pos[:, None]
        scores = scores + slopes[None, :, None, None] * rel[None, None, :, :]
        attn = jax.nn.softmax(scores, axis=-1)
        out = jnp.einsum('bhqk,bkhd->bqhd', attn, V).reshape(bsz, seq_len, EMBED_DIM)
        out = lora_linear(out, Wo, bo, Ao, Bo)
        return x + rezero * out

    def _L0_ffn_ref(x, gate_w, gate_b, w1, b1, w2, b2):
        import jax, jax.numpy as jnp
        import numpy as np
        B, T, C = (4, 256, 128)
        E, H, K = (8, 256, 2)
        b, t, c = x.shape
        xf = x.reshape(b * t, c)
        logits = xf @ gate_w + gate_b
        probs = jax.nn.softmax(logits, axis=-1)
        gates, expert_idx = jax.lax.top_k(probs, K)
        h = jax.nn.relu(jnp.einsum('nc,ech->neh', xf, w1) + b1)
        expert_out = jnp.einsum('neh,ehc->nec', h, w2) + b2
        onehot = jax.nn.one_hot(expert_idx, E, dtype=xf.dtype)
        weights = jnp.einsum('nk,nke->ne', gates, onehot)
        out = jnp.einsum('ne,nec->nc', weights, expert_out)
        return out.reshape(b, t, c)
    x = L0_attn_x
    x = x + _L0_attn_ref(_layernorm(x, axis=-1), L0_attn_Wq, L0_attn_bq, L0_attn_Aq, L0_attn_Bq, L0_attn_Wk, L0_attn_bk, L0_attn_Ak, L0_attn_Bk, L0_attn_Wv, L0_attn_bv, L0_attn_Av, L0_attn_Bv, L0_attn_Wo, L0_attn_bo, L0_attn_Ao, L0_attn_Bo, L0_attn_rezero)
    x = x + _L0_ffn_ref(_layernorm(x, axis=-1), L0_ffn_gate_w, L0_ffn_gate_b, L0_ffn_w1, L0_ffn_b1, L0_ffn_w2, L0_ffn_b2)
    return x

_drawn_inputs = setup_inputs


def setup_inputs(seed=0):
    import zlib

    import numpy as np

    out = dict(_drawn_inputs(seed))
    spreads = {'L0_attn_bq': (0.0, 0.8),
     'L0_attn_bk': (0.0, 2.0),
     'L0_attn_bv': (0.0, 0.8),
     'L0_attn_bo': (0.0, 2.0),
     'L0_ffn_gate_b': (0.0, 0.562)}
    factors = {'L0_attn_Wq': 8.0,
     'L0_attn_Aq': 52.527,
     'L0_attn_Bq': 53.173,
     'L0_attn_Wk': 8.0,
     'L0_attn_Ak': 43.313,
     'L0_attn_Bk': 42.931,
     'L0_attn_Wv': 8.0,
     'L0_attn_Av': 64.0,
     'L0_attn_Bv': 64.0,
     'L0_attn_Wo': 8.0,
     'L0_attn_Ao': 64.0,
     'L0_attn_Bo': 64.0,
     'L0_ffn_b1': 31.439,
     'L0_ffn_b2': 8.0,
     'L0_ffn_w1': 3.036}
    for name, (base, spread) in spreads.items():
        noise = np.random.default_rng([zlib.crc32(name.encode()), seed]).standard_normal(out[name].shape)
        drawn = base * np.exp(spread * noise) if base else spread * noise
        out[name] = jnp.asarray(drawn.astype(out[name].dtype))
    for name, factor in factors.items():
        out[name] = (out[name] * factor).astype(out[name].dtype)
    return out
```

```python
from contextlib import ExitStack

import concourse.bass as bass
from concourse import mybir

F32 = mybir.dt.float32
F32R = mybir.dt.float32r
I32 = mybir.dt.int32
ALU = mybir.AluOpType
ACT = mybir.ActivationFunctionType
AX_X = mybir.AxisListType.X

P = 128
B = 16
S = 512
C = 128
H = 16
D = C // H
R = 8
E = 8
F = 256
TOP = 2
QT = S // P
G = 4
J = H // G
STEPS = G * QT
TILES = STEPS * J
FC = F // P
EPS = 1e-5
LORA_SCALE = 1.0 / R
QK_SCALE = float(1.0 / (D ** 0.5))
RSQRT_SEED = float(0x5F3759DF)

TURN = 2
PRING = 2
SRING = 3
GH = G // 2
PART_ROWS = J * D
POS_ROW = 3 * PART_ROWS
MAX_ROW = POS_ROW + 2 * J
ALL_ROWS = MAX_ROW + 2 * J
STACK_DMAS = 3 + 3 * J
NEWTON = 3


def hold(eng, sem, value, held):
    need(eng, sem, value)
    eng.sem_inc(held, 1)


class Trip:

    def __init__(self, eng, reg):
        self.eng, self.reg, self.gained = eng, reg, {}

    def since(self, sem, per_trip):
        key = (sem.name, per_trip)
        if key not in self.gained:
            self.gained[key] = self.eng.snap(self.reg * per_trip)
        return self.gained[key]


def need(eng, sem, value):
    if isinstance(value, tuple):
        trip, per_trip, plus = value
        assert plus > 0
        with eng.register() as target:
            eng.reg_add(target, trip.since(sem, per_trip), plus)
            eng.wait_ge(sem, target)
    elif value > 0:
        eng.wait_ge(sem, value)


def count(it, per, plus, turn=TURN):
    trip, c = it
    return per * c + plus if trip is None else (trip, turn * per, per * c + plus)


def later(it, n):
    return (it[0], it[1] + n)


def small_uses(i):
    if i == -1:
        return ["xn0", "q0", "k0", "v0", "xn1", "q1", "k1", "maxA"]
    if i == B:
        return ["ctx0", "ctx1", "ctx2", "ctx3", "attn", "out"]
    names = ["maxB"]
    if i + 1 < B:
        names += ["v"]
    if i + 2 < B:
        names += ["xn", "q", "k"]
    if i >= 1:
        names += ["ctx0", "ctx1", "ctx2", "ctx3"]
    if i + 1 < B:
        names += ["maxA"]
    if i >= 1:
        names += ["attn", "out"]
    return names


def small_count(it, name):
    trip, c = it
    n = sum(len(small_uses(i)) for i in range(-1, c)) + small_uses(c).index(name)
    return n if trip is None else (trip, TURN * len(small_uses(TURN)), n)


def then(value, n):
    return value[:2] + (value[2] + n,) if isinstance(value, tuple) else value + n


def chain(eng, step):
    eng.sem_clear(step)
    n = [0]

    def link(ins):
        n[0] += 1
        ins.then_inc(step, 1)
        eng.wait_ge(step, n[0])

    return link


def attention(nc, ctx, d, X1, ffn):
    def sb(name, shape, dt=F32):
        return ctx.enter_context(nc.sbuf_tensor(name, shape, dt))

    def sem(name):
        return ctx.enter_context(nc.semaphore(name))

    ident = ffn["ident"]
    WT = sb("WT", [P, 4, C])
    LA = sb("LA", [R, 4, C])
    LB = sb("LB", [R, 4, C])
    qk_bias = sb("qk_bias", [P, 2])
    bv_all = sb("bv_all", [P, C])
    bo_all = sb("bo_all", [P, C])
    rezero = sb("rezero", [P, 1])
    zeros = sb("zeros", [P, 1])
    x_in = sb("x_in", [P, QT, C])
    stats = sb("stats", [P, QT, 6])
    mv = sb("mv", [P, QT, 2])
    nr = sb("nr", [P, 4, QT])
    xn = sb("xn", [P, QT, C])
    xnT = sb("xnT", [P, S])
    qk_full = [sb("q_full", [P, S]), sb("k_full", [P, S])]
    qk_hi = [sb("q_hi", [P, S], F32R), sb("k_hi", [P, S], F32R)]
    qk_lo = [sb("q_lo", [P, S], F32R), sb("k_lo", [P, S], F32R)]
    Qst = [sb(f"Qst{m}", [P, G, S], F32R) for m in range(TURN)]
    Kst = [ffn["room"], sb("Kst1", [P, J, G, S], F32R)]
    V32 = [sb(f"V32_{m}", [P, QT, H, 32]) for m in range(TURN)]
    w1 = V32[0][:, :, :, :].rearrange("p q h n -> p (q h n)").rearrange("p (e f) -> p e f", f=F)
    rowmax = sb("rowmax", [P, 2, QT, 2 * J])
    nm_hi = [sb(f"nm_hi{h}", [2 * J, S], F32R) for h in range(2)]
    nm_lo = [sb(f"nm_lo{h}", [2 * J, S], F32R) for h in range(2)]
    probs = sb("probs", [P, PRING, J, S])
    ctxT = [sb(f"ctxT{m}", [P, G, S]) for m in range(TURN)]
    inv = sb("inv", [P, QT, H])
    attn = sb("attn", [P, QT, C])
    attnT = sb("attnT", [P, S])
    k_aug = [probs[32 * h:32 * h + ALL_ROWS - POS_ROW, :, :, :] for h in range(2)]
    q_aug = probs[64:64 + MAX_ROW - POS_ROW, 0, :, :]

    PS = ffn["PS"]

    def ring(b, k):
        return (TILES * (b[1] % TURN) + k) % SRING

    def freed(b, k):
        at = ring(b, k)
        if k >= SRING:
            return count(b, TILES, k - SRING + 1)
        before = (None, b[1] + 1)
        last = max(n for n in range(TILES) if ring(before, n) == at)
        return count(b, TILES, last + 1 - TILES)

    sc_bank = lambda b, k: PS[:, ring(b, k), :]
    st_bank = lambda b, k: PS[:, SRING + ring(b, k), :]
    ctx_bank = PS[:, 6, :]
    small = PS[:, 7, :]

    weights_in = sem("weights_in")
    experts_in = sem("experts_in")
    consts_in = sem("consts_in")
    lora_done = sem("lora_done")
    weights_ready = sem("weights_ready")
    v_clear = sem("v_clear")
    k_clear = [sem(f"k{m}_clear") for m in range(TURN)]
    aug_placed = sem("aug_placed")
    x_loaded = sem("x_loaded")
    stats_step = sem("stats_step")
    stats_ready = sem("stats_ready")
    pool_step = sem("pool_step")
    pool_held = sem("pool_held")
    sp_held = sem("sp_held")
    xn_ready = sem("xn_ready")
    qk_split = sem("qk_split")
    stacked = [sem("stackedA"), sem("stackedB")]
    small_filled = sem("small_filled")
    small_emptied = sem("small_emptied")
    negmax_hi = sem("negmax_hi")
    negmax_placed = [sem("negmaxA_placed"), sem("negmaxB_placed")]
    scores_ready = sem("scores_ready")
    max_taken = sem("max_taken")
    st_ready = sem("st_ready")
    probs_ready = sem("probs_ready")
    probs_used = sem("probs_used")
    ctx_copied = sem("ctx_copied")
    inv_ready = sem("inv_ready")

    def rows_of(it):
        trip, c = it
        if trip is None:
            return X1[:, QT * c:QT * (c + 1), :]
        return X1[:, bass.ds(trip.reg * (TURN * QT) + QT * c, QT), :]

    def xn_turned(it):
        trip, c = it
        if trip is None and c < 2:
            return then(small_count((None, -1), f"xn{c}"), 1)
        return then(small_count(later(it, -2), "xn"), 1)

    def projected(it, name):
        trip, c = it
        if trip is None and c < 2:
            return then(small_count((None, -1), f"{name}{c}"), 1)
        return then(small_count(later(it, -2), name), 1)

    hi_copied = sem("hi_copied")
    bias_ready = sem("bias_ready")
    w1_hi_done = sem("w1_hi_done")

    def schedule(eng, iteration):
        iteration((None, 0), 0)
        with eng.Fori(0, TRIPS, 1) as reg:
            trip = Trip(eng, reg)
            for c in range(1, 1 + TURN):
                iteration((trip, c), c)
        for i in range(1 + TURN * TRIPS, B):
            iteration((None, i), i)

    consts_ready = ffn["ident_ready"]
    TRIPS = (B - 4) // TURN

    def head_of(k):
        return (k + 2) % J

    block = ctx.enter_context(nc.Block())
    @block.sync
    def _(sp):
        def load_x(it):
            need(sp, xn_ready, count(it, 1, 0))
            trip, c = it
            src = d["x"][c] if trip is None else d["x"][bass.ds(trip.reg * TURN + c, 1), :, :].rearrange("o t c -> (o t) c")
            sp.dma_start(x_in[:, :, :], src.rearrange("(q p) c -> p q c", p=P)).then_inc(x_loaded, 16)

        def stack(it, half):
            m = it[1] % TURN
            hold(sp, qk_split, count(it, 2, 2), sp_held)
            if it[1] >= TURN:
                need(sp, st_ready, count(later(it, -TURN), TILES, TILES // 2 * (half + 1)))
            groups = slice(GH * half, GH * half + GH)
            rows = GH * PART_ROWS * half
            for n in range(3):
                q_part, k_part = (qk_hi, qk_hi, qk_lo)[n][0], (qk_hi, qk_lo, qk_hi)[n][1]
                r = PART_ROWS * n
                sp.dma_start(Qst[m][r:r + PART_ROWS, groups, :].bitcast(F32),
                             q_part[rows:rows + GH * PART_ROWS, :].bitcast(F32)).then_inc(stacked[half], 16)
                for j in range(J):
                    src = rows + GH * D * j
                    sp.dma_start(Kst[m][r + D * j:r + D * j + D, j, groups, :].bitcast(F32),
                                 k_part[src:src + GH * D, :].bitcast(F32)).then_inc(stacked[half], 16)

        def place_negmax(it, half):
            m = it[1] % TURN
            turned = (later(it, -1), "maxA") if half == 0 else (it, "maxB")
            need(sp, small_emptied, then(small_count(*turned), 1))
            for n, part in enumerate((nm_hi[half], nm_lo[half])):
                r = MAX_ROW + J * n
                sp.dma_start(Qst[m][r:r + J, GH * half:GH * half + GH, :].bitcast(F32), part[:, :].bitcast(F32))\
                  .then_inc(negmax_placed[half], 16)

        load_x((None, 0))
        for n, name in enumerate(("q", "k", "v", "o")):
            sp.dma_start(WT[:, n, :], d[f"W{name}T"]).then_inc(weights_in, 16)
            sp.dma_start(LA[:, n, :], d[f"A{name}"]).then_inc(weights_in, 16)
            sp.dma_start(LB[:, n, :], d[f"B{name}T"]).then_inc(weights_in, 16)
        sp.dma_start(qk_bias[:, :], d["qk_bias"]).then_inc(weights_in, 16)
        sp.dma_start(bv_all[:, :], d["bv"].broadcast_to([P, C])).then_inc(weights_in, 16)
        sp.dma_start(bo_all[:, :], d["bo"].broadcast_to([P, C])).then_inc(weights_in, 16)
        sp.dma_start(rezero[:, :], d["rezero"].broadcast_to([P, 1])).then_inc(weights_in, 16)
        sp.dma_start(q_aug, d["q_aug"]).then_inc(consts_in, 16)
        for h in range(2):
            sp.dma_start(k_aug[h], d["k_aug"][:, 2 * h:2 * h + 2]).then_inc(consts_in, 16)
        sp.wait_ge(consts_in, 16 * 3)
        for m in range(TURN):
            sp.dma_start(Qst[m][POS_ROW:MAX_ROW, :, :].bitcast(F32), q_aug).then_inc(aug_placed, 16)
            for h in range(2):
                sp.dma_start(Kst[m][POS_ROW:ALL_ROWS, 2 * h:2 * h + 2, :, :].bitcast(F32), k_aug[h])\
                  .then_inc(aug_placed, 16)
        load_x((None, 1))
        for m in range(TURN):
            sp.wait_ge(k_clear[m], 1)
            stack((None, m), 0)
            stack((None, m), 1)
            if m == 0:
                load_x((None, 2))
        place_negmax((None, 0), 0)

        def iteration(it, i):
            if 1 <= i < B - 1:
                stack(later(it, 1), 1)
            if i == B - 1:
                sp.wait_ge(probs_used, STEPS * (B - 1))
                sp.dma_start(w1, d["w1"].rearrange("e c h -> c e h")).then_inc(experts_in, 16)
            place_negmax(it, 1)
            if i + 3 < B:
                load_x(later(it, 3))
            if i + 2 < B:
                stack(later(it, 2), 0)
            if i + 1 < B:
                place_negmax(later(it, 1), 0)

        schedule(sp, iteration)

    @block.gpsimd
    def _(pool):
        pool.memset(Kst[0][0:POS_ROW, :, :, :].bitcast(F32), 0.0).then_inc(k_clear[0], 1)
        for m in range(TURN):
            pool.memset(V32[m][:, :, :, :], 0.0).then_inc(v_clear, 1)
        pool.wait_ge(v_clear, TURN)
        for m in range(TURN):
            pool.memset(V32[m][:, :, :, D:D + 1], 1.0).then_inc(v_clear, 1)

        def layer_norm(it):
            link = chain(pool, pool_step)

            hold(pool, stats_ready, count(it, 1, 1), pool_held)
            var, y, a, b = (nr[:, n, :] for n in range(4))
            link(pool.tensor_scalar(var, mv[:, :, 1], EPS, None, ALU.add))
            link(pool.tensor_scalar(y.bitcast(I32), var.bitcast(I32), -0.5, RSQRT_SEED, ALU.mult, ALU.add))
            for _ in range(NEWTON):
                link(pool.tensor_tensor(a, y, y, ALU.mult))
                link(pool.tensor_tensor(b, a, var, ALU.mult))
                link(pool.tensor_scalar(a, b, -0.5, 1.5, ALU.mult, ALU.add))
                link(pool.tensor_tensor(y, y, a, ALU.mult))
            link(pool.tensor_scalar(b, mv[:, :, 0], -1.0, None, ALU.mult))
            if it[1] >= 1:
                hold(pool, small_filled, xn_turned(later(it, -1)), pool_held)
            for q in range(QT):
                last = pool.tensor_scalar(xn[:, q, :], x_in[:, q, :], b[:, q:q + 1], y[:, q:q + 1], ALU.add, ALU.mult)
            link(last)
            X = rows_of(it)
            link(pool.tensor_tensor(X, x_in[:, :, :], xn[:, :, :], ALU.add))
            last = pool.tensor_tensor(X, X, bo_all[:, :].unsqueeze(1).to_broadcast([P, QT, C]), ALU.add)
            last.then_inc(xn_ready, 1)

        def split(it):
            m = it[1] % TURN
            for t in range(2):
                hold(pool, small_emptied, projected(it, "qk"[t]), pool_held)
                if t == 0 and it[1] >= 1:
                    for half in range(2):
                        hold(pool, stacked[half], count(it, 16 * STACK_DMAS, 0), pool_held)
                pool.sem_clear(hi_copied)
                pool.tensor_copy(qk_hi[t][:, :], qk_full[t][:, :]).then_inc(hi_copied, 1)
                pool.wait_ge(hi_copied, 1)
                pool.tensor_tensor(qk_lo[t][:, :], qk_full[t][:, :], qk_hi[t][:, :].bitcast(F32), ALU.subtract)\
                    .then_inc(qk_split, 1)

        pool.wait_ge(bias_ready, 1)
        layer_norm((None, 0))
        layer_norm((None, 1))
        split((None, 0))
        layer_norm((None, 2))
        split((None, 1))
        def iteration(it, i):
            if i + 2 < B:
                split(later(it, 2))
            if i + 3 < B:
                layer_norm(later(it, 3))

        schedule(pool, iteration)
        pool.wait_ge(experts_in, 16 * 3)
        pool.wait_ge(st_ready, TILES * (B - 1))
        pool.tensor_copy(ffn["w1_hi"], w1).then_inc(w1_hi_done, 1)
        pool.wait_ge(w1_hi_done, 1)
        pool.tensor_tensor(ffn["w1_lo"], w1, ffn["w1_hi"].bitcast(F32), ALU.subtract)

    @block.tensor
    def _(pe):
        def fill(it, name, first=False):
            need(pe, small_emptied, small_count(it, name))

        def filled(ins):
            ins.then_inc(small_filled, 1)

        def turn_xn(it, b, name):
            need(pe, xn_ready, count(b, 1, 1))
            fill(it, name)
            for q in range(QT):
                last = pe.transpose(small[:, q * P:(q + 1) * P], xn[:, q, :], ident[:, :])
            filled(last)

        def project_qk(it, name, n):
            fill(it, name)
            filled(pe.matmul(small, WT[:, n, :], xnT[:, :], start=True, stop=True))

        def project_v(it, name):
            fill(it, name)
            for q in range(QT):
                last = pe.matmul(small[:, q * P:(q + 1) * P], xnT[:, q * P:(q + 1) * P], WT[:, 2, :],
                                 start=True, stop=True)
            filled(last)

        def turn_max(it, b, half, name):
            need(pe, max_taken, count(b, TILES, TILES // 2 * (half + 1)))
            fill(it, name)
            for q in range(QT):
                last = pe.transpose(small[0:2 * J, q * P:(q + 1) * P], rowmax[:, half, q, :], ident[:, :])
            filled(last)

        def turn_ctx(it, b, q, name):
            need(pe, ctx_copied, count(b, G, G))
            fill(it, name)
            m = b[1] % TURN
            for g in range(G):
                last = pe.transpose(small[:, g * P:(g + 1) * P], ctxT[m][:, g, q * P:(q + 1) * P], ident[:, :])
            filled(last)

        def turn_attn(it):
            fill(it, "attn")
            for q in range(QT):
                last = pe.transpose(small[:, q * P:(q + 1) * P], attn[:, q, :], ident[:, :])
            filled(last)

        def project_o(it):
            fill(it, "out")
            for q in range(QT):
                last = pe.matmul(small[:, q * P:(q + 1) * P], attnT[:, q * P:(q + 1) * P], WT[:, 3, :],
                                 start=True, stop=True)
            filled(last)

        def score(b, k):
            s, j = k // J, k % J
            g, q = s // QT, s % QT
            m = b[1] % TURN
            need(pe, max_taken, freed(b, k))
            pe.matmul(sc_bank(b, k), Qst[m][0:MAX_ROW, g, q * P:(q + 1) * P], Kst[m][0:MAX_ROW, j, g, :],
                      start=True, stop=True).then_inc(scores_ready, 1)

        def score_t(b, k):
            s, j = k // J, head_of(k)
            g, q = s // QT, s % QT
            m = b[1] % TURN
            need(pe, probs_ready, freed(b, k))
            pe.matmul(st_bank(b, k), Kst[m][0:ALL_ROWS, j, g, q * P:(q + 1) * P], Qst[m][0:ALL_ROWS, g, :],
                      start=True, stop=True).then_inc(st_ready, 1)

        def weigh(b, s):
            g, q = s // QT, s % QT
            m = b[1] % TURN
            need(pe, probs_ready, count(b, TILES, J * (s + 1)))
            if q == 0:
                need(pe, ctx_copied, count(b, G, g))
            for j in range(J):
                last = pe.matmul(ctx_bank[32 * j:32 * j + 32, :], V32[m][:, q, G * g + j, :],
                                 probs[:, s % PRING, j, :], start=(q == 0), stop=(q == QT - 1))
            last.then_inc(probs_used, 1)

        pe.wait_ge(weights_in, 16 * 16)
        for n in range(4):
            last = pe.matmul(small[:, n * C:(n + 1) * C], LA[:, n, :], LB[:, n, :], start=True, stop=True)
        last.then_inc(lora_done, 1)
        pe.wait_ge(consts_ready, 16)
        pe.wait_ge(weights_ready, 3)
        first = (None, -1)
        for b in range(2):
            turn_xn(first, (None, b), f"xn{b}")
            project_qk(first, f"q{b}", 0)
            project_qk(first, f"k{b}", 1)
            if b == 0:
                project_v(first, "v0")
        pe.wait_ge(aug_placed, 16 * 3 * TURN)
        b0 = (None, 0)
        for k in range(TILES):
            if k % (TILES // 2) == 0:
                pe.wait_ge(stacked[k // (TILES // 2)], 16 * STACK_DMAS)
            score(b0, k)
            if k == TILES // 2 + 4:
                turn_max(first, b0, 0, "maxA")

        def iteration(it, i):
            ahead = i + 1 < B
            b1, b2 = later(it, 1), later(it, 2)
            for s in range(STEPS):
                if ahead and s % (STEPS // 2) == 0:
                    need(pe, stacked[s // (STEPS // 2)], count(b1, 16 * STACK_DMAS, 16 * STACK_DMAS))
                if s == 0:
                    turn_max(it, it, 1, "maxB")
                    need(pe, negmax_placed[0], count(it, 16 * 2, 16 * 2))
                if s == 8:
                    need(pe, negmax_placed[1], count(it, 16 * 2, 16 * 2))
                if s == 1 and ahead:
                    project_v(it, "v")
                if i + 2 < B:
                    if s == 2:
                        turn_xn(it, b2, "xn")
                    if s == 3:
                        project_qk(it, "q", 0)
                    if s == 4:
                        project_qk(it, "k", 1)
                if i >= 1:
                    if 5 <= s < 9:
                        turn_ctx(it, later(it, -1), s - 5, f"ctx{s - 5}")
                    if s == 10:
                        turn_attn(it)
                    if s == 11:
                        project_o(it)
                if s == 9 and ahead:
                    turn_max(it, b1, 0, "maxA")
                for j in range(J):
                    if ahead:
                        score(b1, J * s + j)
                    score_t(it, J * s + j)
                if s >= 1:
                    weigh(it, s - 1)
                elif i >= 1:
                    weigh(later(it, -1), STEPS - 1)

        schedule(pe, iteration)
        last = (None, B - 1)
        weigh(last, STEPS - 1)
        end = (None, B)
        for q in range(QT):
            turn_ctx(end, last, q, f"ctx{q}")
        turn_attn(end)
        project_o(end)

    @block.scalar
    def _(act):
        act.dma_start(ident[:, :], d["ident"]).then_inc(consts_ready, 16)
        act.dma_start(ffn["w2"][:, :, :, :], d["w2"].rearrange("e (k p) c -> p e k c", p=P)).then_inc(experts_in, 16)
        act.dma_start(ffn["b1"][:, :], d["b1T"]).then_inc(experts_in, 16)

        def exp_tile(b, k):
            s, j = k // J, head_of(k)
            need(act, st_ready, count(b, TILES, k + 1))
            if k % J == 0:
                need(act, probs_used, count(b, STEPS, s - PRING + 1))
            act.activation(probs[:, s % PRING, j, :], st_bank(b, k), ACT.Exp).then_inc(probs_ready, 1)

        def copy_ctx(b, g):
            need(act, probs_used, count(b, STEPS, QT * (g + 1)))
            act.activation(ctxT[b[1] % TURN][:, g, :], ctx_bank, ACT.Copy).then_inc(ctx_copied, 1)

        def copy_small(it, name, out):
            need(act, small_filled, then(small_count(it, name), 1))
            act.activation(out, small, ACT.Copy).then_inc(small_emptied, 1)

        def copy_qk(it, b, name, t):
            need(act, small_filled, then(small_count(it, name), 1))
            need(act, qk_split, count(b, 2, t - 1))
            act.activation(qk_full[t][:, :], small, ACT.Identity, bias=qk_bias[:, t:t + 1],
                           scale=QK_SCALE if t == 0 else 1.0).then_inc(small_emptied, 1)

        def negate_max(it, b, half, name):
            need(act, small_filled, then(small_count(it, name), 1))
            need(act, negmax_placed[half], count(b, 16 * 2, 0))
            act.activation(nm_hi[half][:, :], small[0:2 * J, :], ACT.Copy, scale=-1.0).then_inc(negmax_hi, 1)

        act.wait_ge(weights_ready, 3)
        first = (None, -1)
        for b in range(2):
            copy_small(first, f"xn{b}", xnT[:, :])
            copy_qk(first, (None, b), f"q{b}", 0)
            copy_qk(first, (None, b), f"k{b}", 1)
        negate_max(first, (None, 0), 0, "maxA")
        act.wait_ge(aug_placed, 16 * 3 * TURN)

        def iteration(it, i):
            b1, b2 = later(it, 1), later(it, 2)
            for s in range(STEPS):
                for j in range(J):
                    if j == 1:
                        if s >= 1 and s % QT == 1 and s > 1:
                            copy_ctx(it, s // QT - 1)
                        if s == 1 and i >= 1:
                            copy_ctx(later(it, -1), G - 1)
                    if j == 2:
                        if s == 0:
                            negate_max(it, it, 1, "maxB")
                        if i + 2 < B:
                            if s == 2:
                                copy_small(it, "xn", xnT[:, :])
                            if s == 3:
                                copy_qk(it, b2, "q", 0)
                            if s == 4:
                                copy_qk(it, b2, "k", 1)
                        if s == 9 and i + 1 < B:
                            negate_max(it, b1, 0, "maxA")
                        if s == 10 and i >= 1:
                            copy_small(it, "attn", attnT[:, :])
                    exp_tile(it, J * s + j)

        schedule(act, iteration)
        copy_ctx((None, B - 1), G - 1)
        copy_small((None, B), "attn", attnT[:, :])

    @block.vector
    def _(dve):
        dve.wait_ge(weights_in, 16 * 16)
        dve.wait_ge(lora_done, 1)
        dve.scalar_tensor_tensor(out=WT[:, :, :], in0=small.rearrange("p (n c) -> p n c", n=4), scalar=LORA_SCALE,
                                 in1=WT[:, :, :], op0=ALU.mult, op1=ALU.add).then_inc(weights_ready, 1)
        dve.tensor_scalar(bo_all[:, :], bo_all[:, :], rezero[:, 0:1], None, ALU.mult).then_inc(bias_ready, 1)
        dve.wait_ge(weights_ready, 1)
        dve.tensor_scalar(WT[:, 3, :], WT[:, 3, :], rezero[:, 0:1], None, ALU.mult).then_inc(weights_ready, 1)
        dve.tensor_scalar(qk_bias[:, 0:1], qk_bias[:, 0:1], QK_SCALE, None, ALU.mult).then_inc(weights_ready, 1)

        def statistics(it):
            dve.sem_clear(stats_step)
            need(dve, x_loaded, count(it, 16, 16))
            need(dve, xn_ready, count(it, 1, 0))
            for q in range(QT):
                last = dve.bn_stats(stats[:, q, :], x_in[:, q, :])
            last.then_inc(stats_step, 1)
            dve.wait_ge(stats_step, 1)
            for q in range(QT):
                last = dve.bn_aggr(mv[:, q, :], stats[:, q:q + 1, :])
            last.then_inc(stats_ready, 1)

        def take_max(b, k):
            s, j = k // J, k % J
            g, q = s // QT, s % QT
            need(dve, scores_ready, count(b, TILES, k + 1))
            col = 2 * j + g % 2
            dve.reduce_max(rowmax[:, g // 2, q, col:col + 1], sc_bank(b, k), AX_X).then_inc(max_taken, 1)

        def place_v(it, b, name):
            need(dve, small_filled, then(small_count(it, name), 1))
            m = b[1] % TURN
            need(dve, probs_used, count(b, STEPS, -STEPS))
            dve.tensor_tensor(V32[m][:, :, :, 0:D], small.rearrange("p (q h d) -> p q h d", q=QT, d=D),
                              bv_all[:, :].rearrange("p (h d) -> p h d", d=D).unsqueeze(1)
                              .to_broadcast([P, QT, H, D]), ALU.add).then_inc(small_emptied, 1)

        def negmax_rest(it, b, half, name):
            need(dve, negmax_hi, count(b, 2, half + 1))
            dve.scalar_tensor_tensor(out=nm_lo[half][:, :], in0=small[0:2 * J, :], scalar=-1.0,
                                     in1=nm_hi[half][:, :].bitcast(F32), op0=ALU.mult, op1=ALU.subtract)\
               .then_inc(small_emptied, 1)

        def scale_ctx(it, b, q, name):
            dve.sem_clear(inv_ready)
            need(dve, small_filled, then(small_count(it, name), 1))
            heads = small.rearrange("p (h r) -> p h r", r=32)
            dve.reciprocal(inv[:, q, :], heads[:, :, D]).then_inc(inv_ready, 1)
            dve.wait_ge(inv_ready, 1)
            dve.tensor_tensor(attn[:, q, :].rearrange("p (h d) -> p h d", d=D), heads[:, :, 0:D],
                              inv[:, q, :].unsqueeze(2).to_broadcast([P, H, D]), ALU.mult)\
               .then_inc(small_emptied, 1)

        def add_out(it, b):
            need(dve, small_filled, then(small_count(it, "out"), 1))
            X = rows_of(b)
            dve.tensor_tensor(X, small.rearrange("p (q c) -> p q c", q=QT), X, ALU.add).then_inc(small_emptied, 1)

        first = (None, -1)
        statistics((None, 0))
        statistics((None, 1))
        dve.wait_ge(v_clear, 2 * TURN)
        place_v(first, (None, 0), "v0")
        dve.memset(Kst[1][0:POS_ROW, :, :, :].bitcast(F32), 0.0).then_inc(k_clear[1], 1)
        statistics((None, 2))
        for k in range(TILES):
            take_max((None, 0), k)
            if k == TILES // 2 + 6:
                negmax_rest(first, (None, 0), 0, "maxA")

        def iteration(it, i):
            b1 = later(it, 1)
            for s in range(STEPS):
                for j in range(J):
                    if j == 2:
                        if s == 0:
                            negmax_rest(it, it, 1, "maxB")
                        if s == 1 and i + 1 < B:
                            place_v(it, later(it, 1), "v")
                        if i >= 1:
                            if 5 <= s < 9:
                                scale_ctx(it, later(it, -1), s - 5, f"ctx{s - 5}")
                            if s == 11:
                                add_out(it, later(it, -1))
                        if s == 9 and i + 1 < B:
                            negmax_rest(it, b1, 0, "maxA")
                        if s == 10 and i + 3 < B:
                            statistics(later(it, 3))
                    if i + 1 < B:
                        take_max(b1, J * s + j)

        schedule(dve, iteration)
        end, last = (None, B), (None, B - 1)
        for q in range(QT):
            scale_ctx(end, last, q, f"ctx{q}")
        add_out(end, last)
        dve.wait_ge(small_emptied, then(small_count(end, "out"), 1))


def experts(nc, ctx, d, X1, ffn, out):
    def sb(name, shape, dt=F32):
        return ctx.enter_context(nc.sbuf_tensor(name, shape, dt))

    def sem(name):
        return ctx.enter_context(nc.semaphore(name))

    ident, PS, w1_hi, w1_lo, w2, b1 = (ffn[n] for n in ("ident", "PS", "w1_hi", "w1_lo", "w2", "b1"))
    HRING, HTRING, YRING = 4, 4, 2
    gate_w = sb("gate_w", [P, E])
    gate_b = sb("gate_b", [P, E])
    b2 = sb("b2", [E, C])
    stats = sb("f_stats", [P, QT, 6])
    mv = sb("f_mv", [P, QT, 2])
    nr = sb("f_nr", [P, 4, QT])
    xn = sb("f_xn", [P, QT, C])
    xT = sb("f_xT", [P, S])
    x_hi = [sb(f"x_hi{m}", [P, S], F32R) for m in range(2)]
    x_lo = [sb(f"x_lo{m}", [P, S], F32R) for m in range(2)]
    logits = sb("logits", [P, QT, E])
    tiny = sb("tiny", [P, 3, QT])
    gates = sb("gates", [P, 2, QT, E])
    beats = sb("beats", [P, QT, E, E])
    rank = sb("rank", [P, QT, E])
    weight = [sb(f"weight{m}", [P, QT, E]) for m in range(2)]
    weightT = sb("weightT", [E, S])
    acc = [sb(f"acc{m}", [P, QT, C]) for m in range(2)]
    hT = sb("hT", [P, HTRING, FC, S])
    h_bank = lambda n: PS[:, n % HRING, :]
    y_bank = lambda n: PS[:, HRING + n % YRING, :]
    small = PS[:, 7, :]

    gate_in = sem("gate_in")
    stats_step = sem("f_stats_step")
    stats_ready = sem("f_stats_ready")
    pool_step = sem("f_pool_step")
    pool_held = sem("f_pool_held")
    logits_ready = sem("logits_ready")
    xn_ready = sem("f_xn_ready")
    small_filled = sem("f_small_filled")
    small_emptied = sem("f_small_emptied")
    x_hi_ready = sem("x_hi_ready")
    x_lo_ready = sem("x_lo_ready")
    exps_ready = sem("exps_ready")
    gate_step = sem("gate_step")
    weight_ready = sem("weight_ready")
    hidden_ready = sem("hidden_ready")
    hT_ready = sem("hT_ready")
    y_ready = sem("y_ready")
    y_added = sem("y_added")
    stored = [sem(f"stored{m}") for m in range(2)]
    beats_clear = sem("beats_clear")

    SMALL = ("xn", "logits", "weight", "bias")
    BIAS_AFTER = 3
    HID = E * FC

    def at(it, per, plus):
        return count(it, per, plus, turn=2)

    def rows_of(it):
        trip, c = it
        if trip is None:
            return X1[:, QT * c:QT * (c + 1), :]
        return X1[:, bass.ds(trip.reg * (2 * QT) + QT * c, QT), :]

    def small_at(it, name):
        return at(it, len(SMALL), SMALL.index(name))

    def schedule(eng, batch):
        for i in range(2):
            batch((None, i), i)
        with eng.Fori(0, B // 2 - 2, 1) as reg:
            trip = Trip(eng, reg)
            for c in range(2, 4):
                batch((trip, c), c)
        for i in range(B - 2, B):
            batch((None, i), i)

    block = ctx.enter_context(nc.Block())

    @block.sync
    def _(sp):
        sp.dma_start(gate_w[:, :], d["gate_w"]).then_inc(gate_in, 16)
        sp.dma_start(gate_b[:, :], d["gate_b"].broadcast_to([P, E])).then_inc(gate_in, 16)
        sp.dma_start(b2[:, :], d["b2"]).then_inc(gate_in, 16)

        def batch(it, i):
            need(sp, y_added, at(it, E, E))
            trip, c = it
            dst = out[c] if trip is None else out[bass.ds(trip.reg * 2 + c, 1), :, :].rearrange("o t c -> (o t) c")
            sp.dma_start(dst.rearrange("(q p) c -> p q c", p=P), acc[c % 2][:, :, :]).then_inc(stored[c % 2], 16)

        schedule(sp, batch)
        for m in range(2):
            sp.wait_ge(stored[m], 16 * B // 2)

    @block.gpsimd
    def _(pool):
        def layer_norm(it):
            link = chain(pool, pool_step)

            hold(pool, stats_ready, at(it, 1, 1), pool_held)
            var, y, a, b = (nr[:, n, :] for n in range(4))
            link(pool.tensor_scalar(var, mv[:, :, 1], EPS, None, ALU.add))
            link(pool.tensor_scalar(y.bitcast(I32), var.bitcast(I32), -0.5, RSQRT_SEED, ALU.mult, ALU.add))
            for _ in range(NEWTON):
                link(pool.tensor_tensor(a, y, y, ALU.mult))
                link(pool.tensor_tensor(b, a, var, ALU.mult))
                link(pool.tensor_scalar(a, b, -0.5, 1.5, ALU.mult, ALU.add))
                link(pool.tensor_tensor(y, y, a, ALU.mult))
            link(pool.tensor_scalar(b, mv[:, :, 0], -1.0, None, ALU.mult))
            hold(pool, small_filled, at(it, len(SMALL), 1 - len(SMALL)), pool_held)
            by_row = lambda v: v.unsqueeze(2).to_broadcast([P, QT, C])
            link(pool.tensor_tensor(xn[:, :, :], rows_of(it), by_row(b), ALU.add))
            pool.tensor_tensor(xn[:, :, :], xn[:, :, :], by_row(y), ALU.mult).then_inc(xn_ready, 1)

        def split(it):
            m = it[1] % 2
            hold(pool, small_emptied, then(small_at(it, "xn"), 1), pool_held)
            hold(pool, hidden_ready, at(it, HID, -HID), pool_held)
            pool.sem_clear(x_hi_ready)
            pool.tensor_copy(x_hi[m][:, :], xT[:, :]).then_inc(x_hi_ready, 1)
            pool.wait_ge(x_hi_ready, 1)
            pool.tensor_tensor(x_lo[m][:, :], xT[:, :], x_hi[m][:, :].bitcast(F32), ALU.subtract)\
                .then_inc(x_lo_ready, 1)

        def prepare(it):
            layer_norm(it)
            split(it)

        prepare((None, 0))

        def batch(it, i):
            if i + 1 < B:
                prepare(later(it, 1))

        schedule(pool, batch)

    @block.scalar
    def _(act):
        def copy_xT(it):
            need(act, small_filled, then(small_at(it, "xn"), 1))
            need(act, x_lo_ready, at(it, 1, 0))
            act.activation(xT[:, :], small, ACT.Copy).then_inc(small_emptied, 1)

        def exp_logits(it):
            need(act, logits_ready, at(it, 1, 1))
            act.activation(gates[:, 0, :, :], logits[:, :, :], ACT.Exp).then_inc(exps_ready, 1)

        def copy_weightT(it):
            need(act, small_filled, then(small_at(it, "weight"), 1))
            act.activation(weightT[:, :], small[0:E, :], ACT.Copy).then_inc(small_emptied, 1)

        def relu(it, e):
            for c in range(FC):
                n = FC * e + c
                need(act, hidden_ready, at(it, HID, n + 1))
                if c == 0:
                    need(act, y_ready, at(it, E, e - HTRING + 1))
                act.activation(hT[:, e % HTRING, c, :], h_bank(n), ACT.Relu,
                               bias=b1[:, n:n + 1]).then_inc(hT_ready, 1)

        copy_xT((None, 0))
        exp_logits((None, 0))

        def batch(it, i):
            nxt = later(it, 1)
            for e in range(E):
                if e == 2:
                    copy_weightT(it)
                if i + 1 < B:
                    if e == 4:
                        copy_xT(nxt)
                    if e == 7:
                        exp_logits(nxt)
                relu(it, e)

        schedule(act, batch)

    @block.vector
    def _(dve):
        dve.memset(beats[:, :, :, :], 0.0).then_inc(beats_clear, 1)
        dve.wait_ge(beats_clear, 1)
        dve.wait_ge(gate_in, 48)

        def statistics(it):
            dve.sem_clear(stats_step)
            X = rows_of(it)
            need(dve, xn_ready, at(it, 1, 0))
            for q in range(QT):
                last = dve.bn_stats(stats[:, q, :], X[:, q, :])
            last.then_inc(stats_step, 1)
            dve.wait_ge(stats_step, 1)
            for q in range(QT):
                last = dve.bn_aggr(mv[:, q, :], stats[:, q:q + 1, :])
            last.then_inc(stats_ready, 1)

        def wide(x):
            return x.unsqueeze(2).to_broadcast([P, QT, E])

        def gate_logits(it):
            link = chain(dve, gate_step)
            need(dve, small_filled, then(small_at(it, "logits"), 1))
            dve.tensor_tensor(logits[:, :, :], small[:, 0:QT * E].rearrange("p (q e) -> p q e", e=E),
                              gate_b[:, :].unsqueeze(1).to_broadcast([P, QT, E]), ALU.add)\
               .then_inc(small_emptied, 1)
            need(dve, small_emptied, then(small_at(it, "logits"), 1))
            link(dve.reduce_max(tiny[:, 0, :], logits[:, :, :], AX_X))
            dve.tensor_tensor(logits[:, :, :], logits[:, :, :], wide(tiny[:, 0, :]), ALU.subtract)\
               .then_inc(logits_ready, 1)

        def gate_probs(it):
            link = chain(dve, gate_step)
            need(dve, exps_ready, at(it, 1, 1))
            link(dve.reduce_sum(tiny[:, 1, :], gates[:, 0, :, :], AX_X))
            link(dve.reciprocal(tiny[:, 2, :], tiny[:, 1, :]))
            link(dve.tensor_tensor(gates[:, 1, :, :], gates[:, 0, :, :], wide(tiny[:, 2, :]), ALU.mult))

        def gate_rank(it):
            p = gates[:, 1, :, :]
            link = chain(dve, gate_step)
            for o in range(E):
                if o + 1 < E:
                    last = dve.tensor_tensor(beats[:, :, o + 1:E, o], p[:, :, o:o + 1].to_broadcast([P, QT, E - o - 1]),
                                             p[:, :, o + 1:E], ALU.is_ge)
                if o > 0:
                    last = dve.tensor_tensor(beats[:, :, 0:o, o], p[:, :, o:o + 1].to_broadcast([P, QT, o]),
                                             p[:, :, 0:o], ALU.is_gt)
            link(last)
            link(dve.reduce_sum(rank[:, :, :], beats[:, :, :, :], AX_X))
            dve.scalar_tensor_tensor(out=weight[it[1] % 2][:, :, :], in0=rank[:, :, :], scalar=float(TOP) - 0.5,
                                     in1=p, op0=ALU.is_lt, op1=ALU.mult).then_inc(weight_ready, 1)

        def add_bias(it):
            m = it[1] % 2
            need(dve, small_filled, then(small_at(it, "bias"), 1))
            need(dve, y_added, at(it, E, BIAS_AFTER))
            dve.tensor_tensor(acc[m][:, :, :], small.rearrange("p (q c) -> p q c", q=QT), acc[m][:, :, :], ALU.add)\
               .then_inc(small_emptied, 1)

        def add_expert(it, e):
            m = it[1] % 2
            need(dve, y_ready, at(it, E, e + 1))
            if e == 0:
                need(dve, weight_ready, at(it, 1, 1))
                need(dve, stored[m], (it[0], 16, 16 * (it[1] // 2)) if it[0] else 16 * (it[1] // 2))
            elif e == BIAS_AFTER:
                need(dve, small_emptied, then(small_at(it, "bias"), 1))
            else:
                need(dve, y_added, at(it, E, e))
            before = acc[m] if e else rows_of(it)
            for q in range(QT):
                last = dve.scalar_tensor_tensor(out=acc[m][:, q, :], in0=y_bank(e)[:, q * C:(q + 1) * C],
                                                scalar=weight[m][:, q, e:e + 1], in1=before[:, q, :],
                                                op0=ALU.mult, op1=ALU.add)
            last.then_inc(y_added, 1)

        first = (None, 0)
        statistics(first)
        gate_logits(first)
        gate_probs(first)
        gate_rank(first)

        def batch(it, i):
            nxt = later(it, 1)
            for e in range(E):
                if e >= 1:
                    add_expert(it, e - 1)
                if e == BIAS_AFTER:
                    add_bias(it)
                if i + 1 < B:
                    if e == 0:
                        statistics(nxt)
                    if e == 6:
                        gate_logits(nxt)
                    if e == 7:
                        gate_probs(nxt)
                        gate_rank(nxt)
            add_expert(it, E - 1)

        schedule(dve, batch)

    @block.tensor
    def _(pe):
        pe.wait_ge(gate_in, 48)

        def filled(ins):
            ins.then_inc(small_filled, 1)

        def turn_xn(it):
            need(pe, xn_ready, at(it, 1, 1))
            need(pe, small_emptied, small_at(it, "xn"))
            for q in range(QT):
                last = pe.transpose(small[:, q * P:(q + 1) * P], xn[:, q, :], ident[:, :])
            filled(last)

        def gate(it):
            need(pe, small_emptied, small_at(it, "logits"))
            for q in range(QT):
                last = pe.matmul(small[:, q * E:(q + 1) * E], xT[:, q * P:(q + 1) * P], gate_w[:, :],
                                 start=True, stop=True)
            filled(last)

        def turn_weight(it):
            need(pe, weight_ready, at(it, 1, 1))
            need(pe, small_emptied, small_at(it, "weight"))
            for q in range(QT):
                last = pe.transpose(small[0:E, q * P:(q + 1) * P], weight[it[1] % 2][:, q, :], ident[:, :])
            filled(last)

        def bias(it):
            need(pe, small_emptied, small_at(it, "bias"))
            for q in range(QT):
                last = pe.matmul(small[:, q * P:(q + 1) * P], weightT[:, q * P:(q + 1) * P], b2[:, :],
                                 start=True, stop=True)
            filled(last)

        def hidden(it, e):
            m = it[1] % 2
            for c in range(FC):
                n = FC * e + c
                need(pe, hT_ready, at(it, HID, n - HRING + 1))
                cols = slice(c * P, (c + 1) * P)
                pe.matmul(h_bank(n), w1_hi[:, e, cols], x_hi[m][:, :], start=True, stop=False)
                pe.matmul(h_bank(n), w1_hi[:, e, cols], x_lo[m][:, :], start=False, stop=False)
                pe.matmul(h_bank(n), w1_lo[:, e, cols], x_hi[m][:, :], start=False, stop=True)\
                  .then_inc(hidden_ready, 1)

        def expert_out(it, e):
            need(pe, hT_ready, at(it, HID, FC * (e + 1)))
            need(pe, y_added, at(it, E, e - YRING + 1))
            for q in range(QT):
                for c in range(FC):
                    last = pe.matmul(y_bank(e)[:, q * C:(q + 1) * C], hT[:, e % HTRING, c, q * P:(q + 1) * P],
                                     w2[:, e, c, :], start=(c == 0), stop=(c == FC - 1))
            last.then_inc(y_ready, 1)

        first = (None, 0)
        turn_xn(first)
        gate(first)

        def batch(it, i):
            nxt = later(it, 1)
            need(pe, x_lo_ready, at(it, 1, 1))
            for e in range(E):
                hidden(it, e)
                if e == 1:
                    turn_weight(it)
                if e == 2:
                    bias(it)
                if e >= 1:
                    expert_out(it, e - 1)
                if i + 1 < B:
                    if e == 3:
                        turn_xn(nxt)
                    if e == 5:
                        gate(nxt)
            expert_out(it, E - 1)

        schedule(pe, batch)


def layer(nc, d, out):
    with ExitStack() as ctx:
        def sb(name, shape, dt=F32):
            return ctx.enter_context(nc.sbuf_tensor(name, shape, dt))

        X1 = sb("X1", [P, B * QT, C])
        ffn = {
            "ident": sb("ident", [P, P]),
            "w2": sb("w2", [P, E, FC, C]),
            "b1": sb("b1", [P, E * FC]),
            "PS": ctx.enter_context(nc.psum_tensor("PS", [P, 8, S], F32)),
            "ident_ready": ctx.enter_context(nc.semaphore("ident_ready")),
        }
        room = sb("room", [P, J, G, S], F32R)
        ffn["room"] = room
        parts = room[:, :, :, :].rearrange("p j g (k n) -> p j (g k) n", n=F)
        ffn["w1_hi"], ffn["w1_lo"] = parts[:, 0], parts[:, 1]
        with ExitStack() as part:
            attention(nc, part, d, X1, ffn)
        with ExitStack() as part:
            experts(nc, part, d, X1, ffn, out)


def _constants():
    import numpy as np

    slopes = 0.5 ** np.arange(H, dtype=np.float32).reshape(G, J).T
    pos = np.arange(S, dtype=np.float32)
    rise = slopes[:, :, None] * pos
    own = np.eye(J, dtype=np.float32)[:, :, None, None]
    q_aug = np.concatenate([np.ones((J, G, S)), -rise])
    k_aug = np.concatenate([own * rise, own * np.ones((J, G, S)),
                            own * np.ones((J, G, S)), own * np.ones((J, G, S))])
    return {"ident": np.eye(P, dtype=np.float32), "q_aug": q_aug.astype(np.float32),
            "k_aug": k_aug.astype(np.float32)}


def kernel(**inputs):
    import numpy as np
    import concourse.bacc as bacc
    from concourse.bass_utils import run_bass_kernel_spmd

    given = {k: np.asarray(v) for k, v in inputs.items()}
    att = lambda n: given["L0_attn_" + n]
    ffn = lambda n: given["L0_ffn_" + n]
    order = np.arange(C).reshape(2, GH, J, D).transpose(0, 2, 3, 1).reshape(C)
    arrays = {"x": att("x"), "rezero": att("rezero").reshape(1, 1)}
    for n in "qkvo":
        pick = order if n in "qk" else np.arange(C)
        arrays[f"W{n}T"] = att("W" + n).T[:, pick]
        arrays[f"A{n}"] = att("A" + n)
        arrays[f"B{n}T"] = att("B" + n).T[:, pick]
    arrays["qk_bias"] = np.stack([att("bq")[order], att("bk")[order]], axis=1)
    arrays["bv"] = att("bv").reshape(1, C)
    arrays["bo"] = att("bo").reshape(1, C)
    arrays["gate_w"] = ffn("gate_w")
    arrays["gate_b"] = ffn("gate_b").reshape(1, E)
    arrays["w1"] = ffn("w1")
    arrays["b1T"] = ffn("b1").reshape(E * FC, P).T
    arrays["w2"] = ffn("w2")
    arrays["b2"] = ffn("b2")
    arrays.update(_constants())

    nc = bacc.Bacc("TRN2", target_bir_lowering=False, num_devices=1)
    d, sent = {}, {}
    for name, a in arrays.items():
        sent["in_" + name] = np.ascontiguousarray(a)
        d[name] = nc.dram_tensor("in_" + name, a.shape, mybir.dt.from_np(a.dtype), kind="ExternalInput").ap()
    out = nc.dram_tensor("out", (B, S, C), F32, kind="ExternalOutput").ap()
    layer(nc, d, out)
    r = run_bass_kernel_spmd(nc, [sent], core_ids=[0])
    return r.results[0]["out"]
```

```python
from contextlib import ExitStack

import concourse.bass as bass
from concourse import mybir

F32 = mybir.dt.float32
F32R = mybir.dt.float32r
I32 = mybir.dt.int32
ALU = mybir.AluOpType
ACT = mybir.ActivationFunctionType
AX_X = mybir.AxisListType.X

P = 128
B = 16
S = 512
C = 128
H = 16
D = C // H
R = 8
E = 8
F = 256
TOP = 2
QT = S // P
G = 4
PAIRS = G // 2
J = H // G
STEPS = G * QT
TILES = STEPS * J
FC = F // P
EPS = 1e-5
LORA_SCALE = 1.0 / R
QK_SCALE = float(1.0 / (D ** 0.5))
RSQRT_SEED = float(0x5F3759DF)

TURN = 2
PRING = 2
SRING = 3
GH = G // 2
PART_ROWS = J * D
POS_ROW = 3 * PART_ROWS
MAX_ROW = POS_ROW + 2 * J
ALL_ROWS = MAX_ROW + 2 * J
STACK_DMAS = 3 + 3 * J
MAX_DMAS = 16 * 2
NEWTON = 3
CTX_STEPS = (7, 11)


def hold(eng, sem, value, held):
    need(eng, sem, value)
    eng.sem_inc(held, 1)


class Trip:

    def __init__(self, eng, reg):
        self.eng, self.reg, self.gained = eng, reg, {}

    def since(self, sem, per_trip):
        key = (sem.name, per_trip)
        if key not in self.gained:
            self.gained[key] = self.eng.snap(self.reg * per_trip)
        return self.gained[key]


def need(eng, sem, value):
    if isinstance(value, tuple):
        trip, per_trip, plus = value
        assert plus > 0
        with eng.register() as target:
            eng.reg_add(target, trip.since(sem, per_trip), plus)
            eng.wait_ge(sem, target)
    elif value > 0:
        eng.wait_ge(sem, value)


def count(it, per, plus, turn=TURN):
    trip, c = it
    return per * c + plus if trip is None else (trip, turn * per, per * c + plus)


def later(it, n):
    return (it[0], it[1] + n)


def small_uses(i):
    if i == -1:
        return ["xn0", "q0", "k0", "v0", "xn1", "q1", "k1", "maxA"]
    if i == B:
        return ["ctx0", "ctx1", "attn", "out"]
    names = ["maxB"]
    if i + 1 < B:
        names += ["v"]
    if i + 2 < B:
        names += ["xn", "q", "k"]
    if i >= 1:
        names += ["ctx0"]
    if i + 1 < B:
        names += ["maxA"]
    if i >= 1:
        names += ["ctx1", "attn", "out"]
    return names


def small_count(it, name):
    trip, c = it
    n = sum(len(small_uses(i)) for i in range(-1, c)) + small_uses(c).index(name)
    return n if trip is None else (trip, TURN * len(small_uses(TURN)), n)


def then(value, n):
    return value[:2] + (value[2] + n,) if isinstance(value, tuple) else value + n


def chain(eng, step):
    eng.sem_clear(step)
    n = [0]

    def link(ins):
        n[0] += 1
        ins.then_inc(step, 1)
        eng.wait_ge(step, n[0])

    return link


def attention(nc, ctx, d, X1, shared):
    def sb(name, shape, dt=F32):
        return ctx.enter_context(nc.sbuf_tensor(name, shape, dt))

    def sem(name):
        return ctx.enter_context(nc.semaphore(name))

    ident = shared["ident"]
    WT = sb("WT", [P, 4, C])
    LA = sb("LA", [R, 4, C])
    LB = sb("LB", [R, 4, C])
    qk_bias = sb("qk_bias", [P, 2])
    bv_all = sb("bv_all", [P, C])
    bo_all = sb("bo_all", [P, C])
    rezero = sb("rezero", [P, 1])
    first_exp = sb("first_exp", [P, 1])
    x_in = shared["x_in"]
    stats = sb("stats", [P, QT, 6])
    mv = sb("mv", [P, QT, 2])
    nr = sb("nr", [P, 4, QT])
    xn = shared["xn"]
    xnT = shared["xnT"]
    qk_full = shared["qk_full"]
    qk_hi = shared["qk_hi"]
    qk_lo = shared["qk_lo"]
    Qst = [sb(f"Qst{m}", [P, G, S], F32R) for m in range(TURN)]
    Kst = [shared["room"], sb("Kst1", [P, J, G, S], F32R)]
    V32 = [sb(f"V32_{m}", [P, QT, H, 32]) for m in range(TURN)]
    w1 = V32[0][:, :, :, :].rearrange("p q h n -> p (q h n)").rearrange("p (e f) -> p e f", f=F)
    rowmax = sb("rowmax", [P, 2, 2 * J, QT])
    nm_hi = [sb(f"nm_hi{h}", [2 * J * QT, P], F32R) for h in range(2)]
    nm_lo = [sb(f"nm_lo{h}", [2 * J * QT, P], F32R) for h in range(2)]
    probs = shared["probs"]
    ctxT = [sb(f"ctxT{m}", [P, PAIRS, S]) for m in range(TURN)]
    inv = sb("inv", [P, QT, H])
    attn = sb("attn", [P, QT, C])
    attnT = sb("attnT", [P, S])
    k_aug = [probs[32 * h:32 * h + ALL_ROWS - POS_ROW, :, :, :] for h in range(2)]
    q_aug = probs[64:64 + MAX_ROW - POS_ROW, 0, :, :]

    PS = shared["PS"]

    def ring(b, k):
        return (TILES * (b[1] % TURN) + k) % SRING

    def freed(b, k):
        at = ring(b, k)
        if k >= SRING:
            return count(b, TILES, k - SRING + 1)
        before = (None, b[1] + 1)
        last = max(n for n in range(TILES) if ring(before, n) == at)
        return count(b, TILES, last + 1 - TILES)

    sc_bank = lambda b, k: PS[:, ring(b, k), :]

    LAST_BANKS = (0, 1, 3, 4, 5)

    def st_bank(b, k):
        if b == (None, B - 1):
            return PS[:, LAST_BANKS[k % len(LAST_BANKS)], :]
        return PS[:, SRING + ring(b, k), :]

    def st_freed(b, k):
        if b != (None, B - 1):
            return freed(b, k)
        n = len(LAST_BANKS)
        return TILES * (B - 1) + (k - n + 1 if k >= n else 0 if k >= 2 else -SRING)

    ctx_bank = PS[:, 6, :]
    small = PS[:, 7, :]

    weights_in = sem("weights_in")
    experts_in = shared["experts_in"]
    consts_in = sem("consts_in")
    lora_done = sem("lora_done")
    weights_ready = sem("weights_ready")
    v_clear = sem("v_clear")
    k_clear = [sem(f"k{m}_clear") for m in range(TURN)]
    aug_placed = sem("aug_placed")
    x_loaded = sem("x_loaded")
    stats_step = sem("stats_step")
    stats_ready = sem("stats_ready")
    pool_step = sem("pool_step")
    pool_held = sem("pool_held")
    sp_held = sem("sp_held")
    normalised = sem("normalised")
    xn_ready = sem("xn_ready")
    qk_split = sem("qk_split")
    stacked = [sem("stackedA"), sem("stackedB")]
    small_filled = sem("small_filled")
    small_emptied = sem("small_emptied")
    negmax_hi = sem("negmax_hi")
    negmax_placed = [sem("negmaxA_placed"), sem("negmaxB_placed")]
    scores_ready = sem("scores_ready")
    max_taken = sem("max_taken")
    st_ready = sem("st_ready")
    probs_ready = sem("probs_ready")
    probs_used = sem("probs_used")
    ctx_copied = sem("ctx_copied")
    inv_ready = sem("inv_ready")

    def rows_of(it):
        trip, c = it
        if trip is None:
            return X1[:, QT * c:QT * (c + 1), :]
        return X1[:, bass.ds(trip.reg * (TURN * QT) + QT * c, QT), :]

    def xn_turned(it):
        trip, c = it
        if trip is None and c < 2:
            return then(small_count((None, -1), f"xn{c}"), 1)
        return then(small_count(later(it, -2), "xn"), 1)

    def projected(it, name):
        trip, c = it
        if trip is None and c < 2:
            return then(small_count((None, -1), f"{name}{c}"), 1)
        return then(small_count(later(it, -2), name), 1)

    hi_copied = sem("hi_copied")
    first_hi = sem("first_hi")
    bias_ready = sem("bias_ready")
    w1_split = shared["w1_split"]

    def schedule(eng, iteration):
        iteration((None, 0), 0)
        with eng.Fori(0, TRIPS, 1) as reg:
            trip = Trip(eng, reg)
            for c in range(1, 1 + TURN):
                iteration((trip, c), c)
        for i in range(1 + TURN * TRIPS, B):
            iteration((None, i), i)

    consts_ready = shared["ident_ready"]
    TRIPS = (B - 4) // TURN

    def head_of(k):
        return (k + 2) % J

    def attention_sync(sp):
        def load_x(it):
            need(sp, xn_ready, count(it, 1, 0))
            trip, c = it
            src = d["x"][c] if trip is None else d["x"][bass.ds(trip.reg * TURN + c, 1), :, :].rearrange("o t c -> (o t) c")
            sp.dma_start(x_in[:, :, :], src.rearrange("(q p) c -> p q c", p=P)).then_inc(x_loaded, 16)

        def stack(it, half):
            m = it[1] % TURN
            if it[1] >= TURN:
                hold(sp, qk_split, count(it, 2, 2), sp_held)
                need(sp, st_ready, count(later(it, -TURN), TILES, TILES // 2 * (half + 1)))
            else:
                sp.wait_ge(qk_split, 2 * it[1] + 1)
            groups = slice(GH * half, GH * half + GH)
            rows = GH * PART_ROWS * half
            for n, part in enumerate((qk_hi[0], qk_hi[0], qk_lo[0])):
                r = PART_ROWS * n
                sp.dma_start(Qst[m][r:r + PART_ROWS, groups, :].bitcast(F32),
                             part[rows:rows + GH * PART_ROWS, :].bitcast(F32)).then_inc(stacked[half], 16)
            if it[1] < TURN:
                sp.wait_ge(qk_split, 2 * it[1] + 2)
            for n, part in enumerate((qk_hi[1], qk_lo[1], qk_hi[1])):
                for j in range(J):
                    r = PART_ROWS * n + D * j
                    src = rows + GH * D * j
                    sp.dma_start(Kst[m][r:r + D, j, groups, :].bitcast(F32),
                                 part[src:src + GH * D, :].bitcast(F32)).then_inc(stacked[half], 16)

        def place_negmax(it, half):
            m = it[1] % TURN
            turned = (later(it, -1), "maxA") if half == 0 else (it, "maxB")
            need(sp, small_emptied, then(small_count(*turned), 1))
            for n, part in enumerate((nm_hi[half], nm_lo[half])):
                r = MAX_ROW + J * n
                sp.dma_start(Qst[m][r:r + J, GH * half:GH * half + GH, :].bitcast(F32), part[:, :].bitcast(F32))\
                  .then_inc(negmax_placed[half], 16)

        load_x((None, 0))
        sp.dma_start(WT[:, :, :], d["WT"].rearrange("n i o -> i n o")).then_inc(weights_in, 16)
        sp.dma_start(LA[:, :, :], d["A"].rearrange("n r i -> r n i")).then_inc(weights_in, 16)
        sp.dma_start(LB[:, :, :], d["BT"].rearrange("n r o -> r n o")).then_inc(weights_in, 16)
        sp.dma_start(qk_bias[:, :], d["qk_bias"]).then_inc(weights_in, 16)
        sp.dma_start(bv_all[:, :], d["bv"].broadcast_to([P, C])).then_inc(weights_in, 16)
        sp.dma_start(bo_all[:, :], d["bo"].broadcast_to([P, C])).then_inc(weights_in, 16)
        sp.dma_start(rezero[:, :], d["rezero"].broadcast_to([P, 1])).then_inc(weights_in, 16)
        sp.dma_start(q_aug, d["q_aug"]).then_inc(consts_in, 16)
        for h in range(2):
            sp.dma_start(k_aug[h], d["k_aug"][:, 2 * h:2 * h + 2]).then_inc(consts_in, 16)
        sp.wait_ge(consts_in, 16 * 3)
        for m in range(TURN):
            sp.dma_start(Qst[m][POS_ROW:MAX_ROW, :, :].bitcast(F32), q_aug).then_inc(aug_placed, 16)
            for h in range(2):
                sp.dma_start(Kst[m][POS_ROW:ALL_ROWS, 2 * h:2 * h + 2, :, :].bitcast(F32), k_aug[h])\
                  .then_inc(aug_placed, 16)
        load_x((None, 1))
        for m in range(TURN):
            sp.wait_ge(k_clear[m], 1)
            stack((None, m), 0)
            if m == 0:
                load_x((None, 2))
            stack((None, m), 1)
        place_negmax((None, 0), 0)

        def iteration(it, i):
            if 1 <= i < B - 1:
                stack(later(it, 1), 1)
            if i == B - 1:
                sp.wait_ge(probs_used, STEPS * (B - 1))
                sp.dma_start(w1, d["w1"].rearrange("e c h -> c e h")).then_inc(experts_in, 16)
            place_negmax(it, 1)
            if i + 3 < B:
                load_x(later(it, 3))
            if i + 2 < B:
                stack(later(it, 2), 0)
            if i + 1 < B:
                place_negmax(later(it, 1), 0)

        schedule(sp, iteration)

    def attention_gpsimd(pool):
        pool.memset(Kst[0][0:POS_ROW, :, :, :].bitcast(F32), 0.0).then_inc(k_clear[0], 1)
        def layer_norm(it):
            link = chain(pool, pool_step)

            hold(pool, stats_ready, count(it, 1, 1), pool_held)
            var, y, a, b = (nr[:, n, :] for n in range(4))
            link(pool.tensor_scalar(var, mv[:, :, 1], EPS, None, ALU.add))
            link(pool.tensor_scalar(y.bitcast(I32), var.bitcast(I32), -0.5, RSQRT_SEED, ALU.mult, ALU.add))
            for _ in range(NEWTON):
                link(pool.tensor_tensor(a, y, y, ALU.mult))
                link(pool.tensor_tensor(b, a, var, ALU.mult))
                link(pool.tensor_scalar(a, b, -0.5, 1.5, ALU.mult, ALU.add))
                link(pool.tensor_tensor(y, y, a, ALU.mult))
            link(pool.tensor_scalar(b, mv[:, :, 0], -1.0, None, ALU.mult))
            if it[1] >= 1:
                hold(pool, small_filled, xn_turned(later(it, -1)), pool_held)
            for q in range(QT):
                last = pool.tensor_scalar(xn[:, q, :], x_in[:, q, :], b[:, q:q + 1], y[:, q:q + 1], ALU.add, ALU.mult)
            last.then_inc(normalised, 1)
            need(pool, normalised, count(it, 1, 1))
            if it[0] is None and it[1] == 0:
                pool.wait_ge(bias_ready, 1)
            X = rows_of(it)
            link(pool.tensor_tensor(X, x_in[:, :, :], xn[:, :, :], ALU.add))
            last = pool.tensor_tensor(X, X, bo_all[:, :].unsqueeze(1).to_broadcast([P, QT, C]), ALU.add)
            last.then_inc(xn_ready, 1)

        def split(it):
            m = it[1] % TURN
            for t in range(2):
                hold(pool, small_emptied, projected(it, "qk"[t]), pool_held)
                if t == 0 and it[1] >= 1:
                    for half in range(2):
                        hold(pool, stacked[half], count(it, 16 * STACK_DMAS, 0), pool_held)
                pool.sem_clear(hi_copied)
                pool.tensor_copy(qk_hi[t][:, :], qk_full[t][:, :]).then_inc(hi_copied, 1)
                pool.wait_ge(hi_copied, 1)
                pool.tensor_tensor(qk_lo[t][:, :], qk_full[t][:, :], qk_hi[t][:, :].bitcast(F32), ALU.subtract)\
                    .then_inc(qk_split, 1)

        layer_norm((None, 0))
        for m in range(TURN):
            pool.memset(V32[m][:, :, :, :], 0.0).then_inc(v_clear, 1)
        pool.wait_ge(v_clear, TURN)
        for m in range(TURN):
            pool.memset(V32[m][:, :, :, D:D + 1], 1.0).then_inc(v_clear, 1)
        layer_norm((None, 1))
        split((None, 1))
        layer_norm((None, 2))

        def iteration(it, i):
            if i + 2 < B:
                split(later(it, 2))
            if i + 3 < B:
                layer_norm(later(it, 3))

        schedule(pool, iteration)
        pool.wait_ge(experts_in, 16 * 3)
        pool.wait_ge(st_ready, TILES * (B - 1))
        pool.tensor_copy(shared["w1_hi"], w1).then_inc(w1_split, 1)
        pool.wait_ge(w1_split, 1)
        pool.tensor_tensor(shared["w1_lo"], w1, shared["w1_hi"].bitcast(F32), ALU.subtract)\
            .then_inc(w1_split, 1)
        for half in range(2):
            pool.wait_ge(stacked[half], 16 * STACK_DMAS * B)

    def attention_tensor(pe, prepare):
        def fill(it, name):
            need(pe, small_emptied, small_count(it, name))

        def filled(ins):
            ins.then_inc(small_filled, 1)

        def turn_xn(it, b, name):
            need(pe, normalised, count(b, 1, 1))
            fill(it, name)
            for q in range(QT):
                last = pe.transpose(small[:, q * P:(q + 1) * P], xn[:, q, :], ident[:, :])
            filled(last)

        def project_qk(it, name, n):
            fill(it, name)
            filled(pe.matmul(small, WT[:, n, :], xnT[:, :], start=True, stop=True))

        def project_v(it, name):
            fill(it, name)
            for q in range(QT):
                last = pe.matmul(small[:, q * P:(q + 1) * P], xnT[:, q * P:(q + 1) * P], WT[:, 2, :],
                                 start=True, stop=True)
            filled(last)

        def turn_max(it, b, half, name):
            need(pe, max_taken, count(b, TILES, TILES // 2 * (half + 1)))
            fill(it, name)
            filled(pe.transpose(small[0:2 * J * QT, 0:P], rowmax[:, half, :, :].rearrange("p n q -> p (n q)"),
                                ident[:, :]))

        def turn_ctx(it, b, u, name):
            need(pe, ctx_copied, count(b, PAIRS, PAIRS))
            fill(it, name)
            m = b[1] % TURN
            for n in range(2 * PAIRS):
                q, a = 2 * u + n // PAIRS, n % PAIRS
                last = pe.transpose(small[:, n * P:(n + 1) * P], ctxT[m][:, a, q * P:(q + 1) * P], ident[:, :])
            filled(last)

        def turn_attn(it):
            fill(it, "attn")
            for q in range(QT):
                last = pe.transpose(small[:, q * P:(q + 1) * P], attn[:, q, :], ident[:, :])
            filled(last)

        def project_o(it):
            fill(it, "out")
            for q in range(QT):
                last = pe.matmul(small[:, q * P:(q + 1) * P], attnT[:, q * P:(q + 1) * P], WT[:, 3, :],
                                 start=True, stop=True)
            filled(last)

        def score(b, k):
            s, j = k // J, k % J
            g, q = s // QT, s % QT
            m = b[1] % TURN
            need(pe, max_taken, freed(b, k))
            pe.matmul(sc_bank(b, k), Qst[m][0:MAX_ROW, g, q * P:(q + 1) * P], Kst[m][0:MAX_ROW, j, g, :],
                      start=True, stop=True).then_inc(scores_ready, 1)

        def score_t(b, k):
            s, j = k // J, head_of(k)
            g, q = s // QT, s % QT
            m = b[1] % TURN
            need(pe, probs_ready, st_freed(b, k))
            pe.matmul(st_bank(b, k), Kst[m][0:ALL_ROWS, j, g, q * P:(q + 1) * P], Qst[m][0:ALL_ROWS, g, :],
                      start=True, stop=True).then_inc(st_ready, 1)

        def weigh(b, s):
            g, q = s // QT, s % QT
            m = b[1] % TURN
            need(pe, probs_ready, count(b, TILES, J * (s + 1)))
            first, last_one = q == 0 and g % 2 == 0, q == QT - 1 and g % 2 == 1
            if first:
                need(pe, ctx_copied, count(b, PAIRS, g // 2))
            values = V32[m][:, q, :, :].rearrange("p h n -> p (h n)")
            for j in range(J):
                at = 32 * (J * g + j) - 16 * (g % 2)
                last = pe.matmul(ctx_bank[32 * j:32 * j + 32, :], values[:, at:at + 32],
                                 probs[:, s % PRING, j, :], start=first, stop=last_one)
            last.then_inc(probs_used, 1)

        pe.wait_ge(weights_in, 16 * 7)
        for n in range(4):
            last = pe.matmul(small[:, n * C:(n + 1) * C], LA[:, n, :], LB[:, n, :], start=True, stop=True)
        last.then_inc(lora_done, 1)
        pe.wait_ge(consts_ready, 16)
        pe.wait_ge(weights_ready, 3)
        first = (None, -1)
        for b in range(2):
            turn_xn(first, (None, b), f"xn{b}")
            project_qk(first, f"q{b}", 0)
            project_qk(first, f"k{b}", 1)
            if b == 0:
                project_v(first, "v0")
        pe.wait_ge(aug_placed, 16 * 3 * TURN)
        b0 = (None, 0)
        for k in range(TILES):
            if k % (TILES // 2) == 0:
                pe.wait_ge(stacked[k // (TILES // 2)], 16 * STACK_DMAS)
            score(b0, k)
            if k == TILES // 2 + 4:
                turn_max(first, b0, 0, "maxA")

        def iteration(it, i):
            ahead = i + 1 < B
            b1, b2 = later(it, 1), later(it, 2)
            for s in range(STEPS):
                if ahead and s % (STEPS // 2) == 0:
                    need(pe, stacked[s // (STEPS // 2)], count(b1, 16 * STACK_DMAS, 16 * STACK_DMAS))
                if s == 1:
                    turn_max(it, it, 1, "maxB")
                if s == 0 and not ahead:
                    need(pe, max_taken, TILES * B)
                if s == 0:
                    need(pe, negmax_placed[0], count(it, MAX_DMAS, MAX_DMAS))
                if s == 8:
                    need(pe, negmax_placed[1], count(it, MAX_DMAS, MAX_DMAS))
                if s == 3 and ahead:
                    project_v(it, "v")
                if i + 2 < B:
                    if s == 4:
                        turn_xn(it, b2, "xn")
                    if s == 5:
                        project_qk(it, "q", 0)
                    if s == 6:
                        project_qk(it, "k", 1)
                if i >= 1:
                    if s in CTX_STEPS:
                        u = CTX_STEPS.index(s)
                        turn_ctx(it, later(it, -1), u, f"ctx{u}")
                    if s == 13:
                        turn_attn(it)
                    if s == 14:
                        project_o(it)
                if s == 9 and ahead:
                    turn_max(it, b1, 0, "maxA")
                for j in range(J):
                    if ahead:
                        score(b1, J * s + j)
                    score_t(it, J * s + j)
                if s >= 1:
                    weigh(it, s - 1)
                elif i >= 1:
                    weigh(later(it, -1), STEPS - 1)
                if not ahead:
                    prepare(s)

        schedule(pe, iteration)
        last = (None, B - 1)
        weigh(last, STEPS - 1)
        end = (None, B)

        def tail(e):
            if e < 2:
                turn_ctx(end, last, e, f"ctx{e}")
            if e == 2:
                turn_attn(end)
            if e == 3:
                project_o(end)

        return tail

    def attention_scalar(act, prepare):
        act.dma_start(ident[:, :], d["ident"]).then_inc(consts_ready, 16)

        def exp_tile(b, k):
            s, j = k // J, head_of(k)
            need(act, st_ready, count(b, TILES, k + 1))
            if k % J == 0:
                need(act, probs_used, count(b, STEPS, s - PRING + 1))
            act.activation(probs[:, s % PRING, j, :], st_bank(b, k), ACT.Exp).then_inc(probs_ready, 1)

        def copy_ctx(b, a):
            need(act, probs_used, count(b, STEPS, 2 * QT * (a + 1)))
            act.activation(ctxT[b[1] % TURN][:, a, :], ctx_bank, ACT.Copy).then_inc(ctx_copied, 1)

        def copy_small(it, name, out):
            need(act, small_filled, then(small_count(it, name), 1))
            act.activation(out, small, ACT.Copy).then_inc(small_emptied, 1)

        def copy_qk(it, b, name, t):
            need(act, small_filled, then(small_count(it, name), 1))
            need(act, qk_split, count(b, 2, t - 1))
            act.activation(qk_full[t][:, :], small, ACT.Identity, bias=qk_bias[:, t:t + 1],
                           scale=QK_SCALE if t == 0 else 1.0).then_inc(small_emptied, 1)

        def negate_max(it, b, half, name):
            need(act, small_filled, then(small_count(it, name), 1))
            need(act, negmax_placed[half], count(b, MAX_DMAS, 0))
            act.activation(nm_hi[half][:, :], small[0:2 * J * QT, 0:P], ACT.Copy, scale=-1.0).then_inc(negmax_hi, 1)

        act.wait_ge(consts_ready, 16)
        act.activation(first_exp[:, :], ident[:, 0:1], ACT.Exp)
        act.wait_ge(weights_ready, 3)
        first = (None, -1)
        for b in range(2):
            copy_small(first, f"xn{b}", xnT[:, :])
            copy_qk(first, (None, b), f"q{b}", 0)
            copy_qk(first, (None, b), f"k{b}", 1)
        act.dma_start(shared["w2"][:, :, :, :], d["w2"].rearrange("e (k p) c -> p e k c", p=P)).then_inc(experts_in, 16)
        act.dma_start(shared["b1"][:, :], d["b1T"]).then_inc(experts_in, 16)
        negate_max(first, (None, 0), 0, "maxA")
        act.wait_ge(aug_placed, 16 * 3 * TURN)

        def iteration(it, i):
            b1, b2 = later(it, 1), later(it, 2)
            for s in range(STEPS):
                for j in range(J):
                    if j == 1:
                        if s == 2 * QT + 1:
                            copy_ctx(it, 0)
                        if s == 1 and i >= 1:
                            copy_ctx(later(it, -1), 1)
                    if j == 2:
                        if s == 1:
                            negate_max(it, it, 1, "maxB")
                        if i + 2 < B:
                            if s == 4:
                                copy_small(it, "xn", xnT[:, :])
                            if s == 5:
                                copy_qk(it, b2, "q", 0)
                            if s == 6:
                                copy_qk(it, b2, "k", 1)
                        if s == 9 and i + 1 < B:
                            negate_max(it, b1, 0, "maxA")
                        if s == 13 and i >= 1:
                            copy_small(it, "attn", attnT[:, :])
                    exp_tile(it, J * s + j)
                if i == B - 1:
                    prepare(s)

        schedule(act, iteration)
        copy_ctx((None, B - 1), 1)

        def tail(e):
            if e == 2:
                copy_small((None, B), "attn", attnT[:, :])

        return tail

    def attention_vector(dve, prepare):
        def statistics(it):
            dve.sem_clear(stats_step)
            need(dve, x_loaded, count(it, 16, 16))
            need(dve, xn_ready, count(it, 1, 0))
            for q in range(QT):
                last = dve.bn_stats(stats[:, q, :], x_in[:, q, :])
            last.then_inc(stats_step, 1)
            dve.wait_ge(stats_step, 1)
            for q in range(QT):
                last = dve.bn_aggr(mv[:, q, :], stats[:, q:q + 1, :])
            last.then_inc(stats_ready, 1)

        def take_max(b, k):
            s, j = k // J, k % J
            g, q = s // QT, s % QT
            need(dve, scores_ready, count(b, TILES, k + 1))
            col = 2 * j + g % 2
            dve.reduce_max(rowmax[:, g // 2, col, q:q + 1], sc_bank(b, k), AX_X).then_inc(max_taken, 1)

        def place_v(it, b, name):
            need(dve, small_filled, then(small_count(it, name), 1))
            m = b[1] % TURN
            need(dve, probs_used, count(b, STEPS, -STEPS))
            dve.tensor_tensor(V32[m][:, :, :, 0:D], small.rearrange("p (q h d) -> p q h d", q=QT, d=D),
                              bv_all[:, :].rearrange("p (h d) -> p h d", d=D).unsqueeze(1)
                              .to_broadcast([P, QT, H, D]), ALU.add).then_inc(small_emptied, 1)

        def negmax_rest(it, b, half, name):
            need(dve, negmax_hi, count(b, 2, half + 1))
            dve.scalar_tensor_tensor(out=nm_lo[half][:, :], in0=small[0:2 * J * QT, 0:P], scalar=-1.0,
                                     in1=nm_hi[half][:, :].bitcast(F32), op0=ALU.mult, op1=ALU.subtract)\
               .then_inc(small_emptied, 1)

        def scale_ctx(it, b, u, name):
            dve.sem_clear(inv_ready)
            need(dve, small_filled, then(small_count(it, name), 1))
            heads = small.rearrange("p (h r) -> p h r", r=16)
            recip = inv[:, 2 * u:2 * u + 2, :].rearrange("p q h -> p (q h)")
            dve.reciprocal(recip, heads[:, :, D]).then_inc(inv_ready, 1)
            dve.wait_ge(inv_ready, 1)
            dve.tensor_tensor(attn[:, 2 * u:2 * u + 2, :].rearrange("p q (h d) -> p (q h) d", d=D), heads[:, :, 0:D],
                              recip.unsqueeze(2).to_broadcast([P, 2 * H, D]), ALU.mult)\
               .then_inc(small_emptied, 1)

        def add_out(it, b):
            need(dve, small_filled, then(small_count(it, "out"), 1))
            X = rows_of(b)
            dve.tensor_tensor(X, small.rearrange("p (q c) -> p q c", q=QT), X, ALU.add).then_inc(small_emptied, 1)

        first = (None, -1)
        statistics((None, 0))
        dve.wait_ge(weights_in, 16 * 7)
        dve.wait_ge(lora_done, 1)
        dve.scalar_tensor_tensor(out=WT[:, :, :], in0=small.rearrange("p (n c) -> p n c", n=4), scalar=LORA_SCALE,
                                 in1=WT[:, :, :], op0=ALU.mult, op1=ALU.add).then_inc(weights_ready, 1)
        dve.tensor_scalar(bo_all[:, :], bo_all[:, :], rezero[:, 0:1], None, ALU.mult).then_inc(bias_ready, 1)
        dve.wait_ge(weights_ready, 1)
        dve.tensor_scalar(WT[:, 3, :], WT[:, 3, :], rezero[:, 0:1], None, ALU.mult).then_inc(weights_ready, 1)
        dve.tensor_scalar(qk_bias[:, 0:1], qk_bias[:, 0:1], QK_SCALE, None, ALU.mult).then_inc(weights_ready, 1)
        dve.memset(Kst[1][0:POS_ROW, :, :, :].bitcast(F32), 0.0).then_inc(k_clear[1], 1)
        for t in range(2):
            need(dve, small_emptied, then(small_count(first, f"{'qk'[t]}0"), 1))
            dve.tensor_copy(qk_hi[t][:, :], qk_full[t][:, :]).then_inc(first_hi, 1)
            dve.wait_ge(first_hi, t + 1)
            dve.tensor_tensor(qk_lo[t][:, :], qk_full[t][:, :], qk_hi[t][:, :].bitcast(F32), ALU.subtract)\
               .then_inc(qk_split, 1)
            if t == 0:
                statistics((None, 1))
        dve.wait_ge(v_clear, 2 * TURN)
        place_v(first, (None, 0), "v0")
        for k in range(TILES):
            if k == TILES // 4:
                statistics((None, 2))
            take_max((None, 0), k)
            if k == TILES // 2 + 6:
                negmax_rest(first, (None, 0), 0, "maxA")

        def iteration(it, i):
            b1 = later(it, 1)
            for s in range(STEPS):
                for j in range(J):
                    if j == 2:
                        if s == 2:
                            negmax_rest(it, it, 1, "maxB")
                        if s == 3 and i + 1 < B:
                            place_v(it, later(it, 1), "v")
                        if i >= 1:
                            if s in CTX_STEPS:
                                u = CTX_STEPS.index(s)
                                scale_ctx(it, later(it, -1), u, f"ctx{u}")
                            if s == 14:
                                add_out(it, later(it, -1))
                        if s == 10 and i + 1 < B:
                            negmax_rest(it, b1, 0, "maxA")
                        if s == 5 and i + 3 < B:
                            statistics(later(it, 3))
                    if i + 1 < B:
                        take_max(b1, J * s + j)
                if i == B - 1:
                    prepare(s)

        schedule(dve, iteration)
        end, last = (None, B), (None, B - 1)

        def tail(e):
            if e < 2:
                scale_ctx(end, last, e, f"ctx{e}")
            if e == 4:
                add_out(end, last)

        return tail

    return attention_sync, attention_gpsimd, attention_tensor, attention_scalar, attention_vector


def experts(nc, ctx, d, X1, shared, out):
    def sb(name, shape, dt=F32):
        return ctx.enter_context(nc.sbuf_tensor(name, shape, dt))

    def sem(name):
        return ctx.enter_context(nc.semaphore(name))

    ident, PS, w1_hi, w1_lo, w2, b1 = (shared[n] for n in ("ident", "PS", "w1_hi", "w1_lo", "w2", "b1"))
    HRING, HTRING, YRING = 4, PRING * J // FC, 2
    gate_w = sb("gate_w", [P, E])
    gate_b = sb("gate_b", [P, E])
    b2 = sb("b2", [P, E, C])
    stats = sb("f_stats", [P, QT, 6])
    mv = sb("f_mv", [P, QT, 2])
    nr = sb("f_nr", [P, 4, QT])
    xn, xT, x_hi, x_lo = (shared[n] for n in ("xn", "xnT", "qk_hi", "qk_lo"))
    hT = shared["probs"][:, :, :, :].rearrange("p a (b k) n -> p (a b) k n", k=FC)
    logits = sb("logits", [P, QT, E])
    tiny = sb("tiny", [P, 3, QT])
    free = shared["x_in"][:, :, :].rearrange("p q c -> p (q c)")
    beats = free[:, 0:QT * E * E].rearrange("p (q e o) -> p q e o", q=QT, e=E)
    gates = free[:, QT * E * E:QT * E * (E + 2)].rearrange("p (n q e) -> p n q e", n=2, e=E)
    rank = sb("rank", [P, QT, E])
    weight = [sb(f"weight{m}", [P, QT, E]) for m in range(2)]
    acc = [t[:, :].rearrange("p (q c) -> p q c", q=QT) for t in shared["qk_full"]]
    small = PS[:, 2, :]
    h_bank = lambda n: PS[:, (0, 1, 3, 4)[n % HRING], :]
    y_bank = lambda n: PS[:, (5, 6)[n % YRING], :]

    gate_in = sem("gate_in")
    stats_step = sem("f_stats_step")
    stats_ready = sem("f_stats_ready")
    pool_step = sem("f_pool_step")
    pool_held = sem("f_pool_held")
    logits_ready = sem("logits_ready")
    xn_ready = sem("f_xn_ready")
    small_filled = sem("f_small_filled")
    small_emptied = sem("f_small_emptied")
    x_hi_ready = sem("x_hi_ready")
    x_lo_ready = sem("x_lo_ready")
    exps_ready = sem("exps_ready")
    gate_step = sem("gate_step")
    weight_ready = sem("weight_ready")
    hidden_ready = sem("hidden_ready")
    hT_ready = sem("hT_ready")
    y_ready = sem("y_ready")
    y_added = sem("y_added")
    bias_added = sem("bias_added")
    stored = [sem(f"stored{m}") for m in range(2)]
    beats_clear = sem("beats_clear")

    SMALL = ("xn", "logits")
    HID = E * FC

    def at(it, per, plus):
        return count(it, per, plus, turn=2)

    def rows_of(it):
        trip, c = it
        if trip is None:
            return X1[:, QT * c:QT * (c + 1), :]
        return X1[:, bass.ds(trip.reg * (2 * QT) + QT * c, QT), :]

    def small_at(it, name):
        return at(it, len(SMALL), SMALL.index(name))

    def schedule(eng, batch):
        for i in range(2):
            batch((None, i), i)
        with eng.Fori(0, B // 2 - 2, 1) as reg:
            trip = Trip(eng, reg)
            for c in range(2, 4):
                batch((trip, c), c)
        for i in range(B - 2, B):
            batch((None, i), i)

    def experts_sync(sp):
        sp.dma_start(gate_w[:, :], d["gate_w"]).then_inc(gate_in, 16)
        sp.dma_start(gate_b[:, :], d["gate_b"].broadcast_to([P, E])).then_inc(gate_in, 16)
        sp.dma_start(b2[:, :, :].rearrange("p e c -> p (e c)"), d["b2"].broadcast_to([P, E * C])).then_inc(gate_in, 16)

        def batch(it, i):
            need(sp, bias_added, at(it, E, E))
            trip, c = it
            dst = out[c] if trip is None else out[bass.ds(trip.reg * 2 + c, 1), :, :].rearrange("o t c -> (o t) c")
            sp.dma_start(dst.rearrange("(q p) c -> p q c", p=P), acc[c % 2][:, :, :]).then_inc(stored[c % 2], 16)

        schedule(sp, batch)
        for m in range(2):
            sp.wait_ge(stored[m], 16 * B // 2)

    def experts_gpsimd(pool):
        def layer_norm(it):
            link = chain(pool, pool_step)

            hold(pool, stats_ready, at(it, 1, 1), pool_held)
            var, y, a, b = (nr[:, n, :] for n in range(4))
            link(pool.tensor_scalar(var, mv[:, :, 1], EPS, None, ALU.add))
            link(pool.tensor_scalar(y.bitcast(I32), var.bitcast(I32), -0.5, RSQRT_SEED, ALU.mult, ALU.add))
            for _ in range(NEWTON):
                link(pool.tensor_tensor(a, y, y, ALU.mult))
                link(pool.tensor_tensor(b, a, var, ALU.mult))
                link(pool.tensor_scalar(a, b, -0.5, 1.5, ALU.mult, ALU.add))
                link(pool.tensor_tensor(y, y, a, ALU.mult))
            link(pool.tensor_scalar(b, mv[:, :, 0], -1.0, None, ALU.mult))
            hold(pool, small_filled, at(it, len(SMALL), 1 - len(SMALL)), pool_held)
            by_row = lambda v: v.unsqueeze(2).to_broadcast([P, QT, C])
            link(pool.tensor_tensor(xn[:, :, :], rows_of(it), by_row(b), ALU.add))
            pool.tensor_tensor(xn[:, :, :], xn[:, :, :], by_row(y), ALU.mult).then_inc(xn_ready, 1)

        def split(it):
            m = it[1] % 2
            hold(pool, small_emptied, then(small_at(it, "xn"), 1), pool_held)
            hold(pool, hidden_ready, at(it, HID, -HID), pool_held)
            pool.sem_clear(x_hi_ready)
            pool.tensor_copy(x_hi[m][:, :], xT[:, :]).then_inc(x_hi_ready, 1)
            pool.wait_ge(x_hi_ready, 1)
            pool.tensor_tensor(x_lo[m][:, :], xT[:, :], x_hi[m][:, :].bitcast(F32), ALU.subtract)\
                .then_inc(x_lo_ready, 1)

        def prepare(it):
            layer_norm(it)
            split(it)

        prepare((None, 0))

        def batch(it, i):
            if i + 1 < B:
                prepare(later(it, 1))

        schedule(pool, batch)

    def experts_scalar(act):
        def copy_xT(it):
            need(act, small_filled, then(small_at(it, "xn"), 1))
            need(act, x_lo_ready, at(it, 1, 0))
            act.activation(xT[:, :], small, ACT.Copy).then_inc(small_emptied, 1)

        def exp_logits(it):
            need(act, logits_ready, at(it, 1, 1))
            act.activation(gates[:, 0, :, :], logits[:, :, :], ACT.Exp).then_inc(exps_ready, 1)

        def relu(it, e):
            for c in range(FC):
                n = FC * e + c
                need(act, hidden_ready, at(it, HID, n + 1))
                if c == 0:
                    need(act, y_ready, at(it, E, e - HTRING + 1))
                act.activation(hT[:, e % HTRING, c, :], h_bank(n), ACT.Relu,
                               bias=b1[:, n:n + 1]).then_inc(hT_ready, 1)

        def prepare(s):
            if s == 12:
                copy_xT((None, 0))
            if s == 15:
                exp_logits((None, 0))

        def batch(it, i):
            nxt = later(it, 1)
            for e in range(E):
                if i + 1 < B:
                    if e == 5:
                        copy_xT(nxt)
                relu(it, e)
                if e == E - 1 and i + 1 < B:
                    exp_logits(nxt)
                if i == 0:
                    tail_of[0](e)

        def run(tail):
            tail_of.append(tail)
            act.wait_ge(shared["experts_in"], 16 * 3)
            schedule(act, batch)

        tail_of = []
        return prepare, run

    def experts_vector(dve):
        def statistics(it):
            dve.sem_clear(stats_step)
            X = rows_of(it)
            need(dve, xn_ready, at(it, 1, 0))
            for q in range(QT):
                last = dve.bn_stats(stats[:, q, :], X[:, q, :])
            last.then_inc(stats_step, 1)
            dve.wait_ge(stats_step, 1)
            for q in range(QT):
                last = dve.bn_aggr(mv[:, q, :], stats[:, q:q + 1, :])
            last.then_inc(stats_ready, 1)

        def wide(x):
            return x.unsqueeze(2).to_broadcast([P, QT, E])

        def gate_logits(it):
            link = chain(dve, gate_step)
            need(dve, small_filled, then(small_at(it, "logits"), 1))
            dve.tensor_tensor(logits[:, :, :], small[:, 0:QT * E].rearrange("p (q e) -> p q e", e=E),
                              gate_b[:, :].unsqueeze(1).to_broadcast([P, QT, E]), ALU.add)\
               .then_inc(small_emptied, 1)
            need(dve, small_emptied, then(small_at(it, "logits"), 1))
            link(dve.reduce_max(tiny[:, 0, :], logits[:, :, :], AX_X))
            dve.tensor_tensor(logits[:, :, :], logits[:, :, :], wide(tiny[:, 0, :]), ALU.subtract)\
               .then_inc(logits_ready, 1)

        def gate_probs(it):
            link = chain(dve, gate_step)
            need(dve, exps_ready, at(it, 1, 1))
            link(dve.reduce_sum(tiny[:, 1, :], gates[:, 0, :, :], AX_X))
            link(dve.reciprocal(tiny[:, 2, :], tiny[:, 1, :]))
            link(dve.tensor_tensor(gates[:, 1, :, :], gates[:, 0, :, :], wide(tiny[:, 2, :]), ALU.mult))

        def gate_rank(it):
            p = gates[:, 1, :, :]
            link = chain(dve, gate_step)
            for o in range(E):
                if o + 1 < E:
                    last = dve.tensor_tensor(beats[:, :, o + 1:E, o], p[:, :, o:o + 1].to_broadcast([P, QT, E - o - 1]),
                                             p[:, :, o + 1:E], ALU.is_ge)
                if o > 0:
                    last = dve.tensor_tensor(beats[:, :, 0:o, o], p[:, :, o:o + 1].to_broadcast([P, QT, o]),
                                             p[:, :, 0:o], ALU.is_gt)
            link(last)
            link(dve.reduce_sum(rank[:, :, :], beats[:, :, :, :], AX_X))
            dve.scalar_tensor_tensor(out=weight[it[1] % 2][:, :, :], in0=rank[:, :, :], scalar=float(TOP) - 0.5,
                                     in1=p, op0=ALU.is_lt, op1=ALU.mult).then_inc(weight_ready, 1)

        def add_expert(it, e):
            m = it[1] % 2
            need(dve, y_ready, at(it, E, e + 1))
            if e == 0:
                need(dve, weight_ready, at(it, 1, 1))
                need(dve, stored[m], (it[0], 16, 16 * (it[1] // 2)) if it[0] else 16 * (it[1] // 2))
            else:
                need(dve, bias_added, at(it, E, e))
            before = acc[m] if e else rows_of(it)
            for q in range(QT):
                last = dve.scalar_tensor_tensor(out=acc[m][:, q, :], in0=y_bank(e)[:, q * C:(q + 1) * C],
                                                scalar=weight[m][:, q, e:e + 1], in1=before[:, q, :],
                                                op0=ALU.mult, op1=ALU.add)
            last.then_inc(y_added, 1)
            need(dve, y_added, at(it, E, e + 1))
            for q in range(QT):
                last = dve.scalar_tensor_tensor(out=acc[m][:, q, :], in0=b2[:, e, :],
                                                scalar=weight[m][:, q, e:e + 1], in1=acc[m][:, q, :],
                                                op0=ALU.mult, op1=ALU.add)
            last.then_inc(bias_added, 1)

        first = (None, 0)

        def prepare(s):
            if s == 4:
                statistics(first)
            if s == 15:
                dve.memset(beats[:, :, :, :], 0.0).then_inc(beats_clear, 1)
                dve.wait_ge(beats_clear, 1)
                dve.wait_ge(gate_in, 48)
                statistics(later(first, 1))
                gate_logits(first)
                gate_probs(first)
                gate_rank(first)

        def batch(it, i):
            nxt = later(it, 1)
            for e in range(E):
                if i == 0:
                    tail_of[0](e)
                if e >= 1:
                    add_expert(it, e - 1)
                elif i >= 1:
                    add_expert(later(it, -1), E - 1)
                    gate_probs(it)
                    gate_rank(it)
                if i + 1 < B:
                    if e == 5 and i + 2 < B:
                        statistics(later(it, 2))
                    if e == 6:
                        gate_logits(nxt)

        def run(tail):
            tail_of.append(tail)
            schedule(dve, batch)
            add_expert((None, B - 1), E - 1)

        tail_of = []
        return prepare, run

    def experts_tensor(pe):
        def filled(ins):
            ins.then_inc(small_filled, 1)

        def turn_xn(it):
            need(pe, xn_ready, at(it, 1, 1))
            need(pe, small_emptied, small_at(it, "xn"))
            for q in range(QT):
                last = pe.transpose(small[:, q * P:(q + 1) * P], xn[:, q, :], ident[:, :])
            filled(last)

        def gate(it):
            need(pe, small_emptied, small_at(it, "logits"))
            for q in range(QT):
                last = pe.matmul(small[:, q * E:(q + 1) * E], xT[:, q * P:(q + 1) * P], gate_w[:, :],
                                 start=True, stop=True)
            filled(last)

        def hidden(it, e):
            m = it[1] % 2
            for c in range(FC):
                n = FC * e + c
                need(pe, hT_ready, at(it, HID, n - HRING + 1))
                cols = slice(c * P, (c + 1) * P)
                pe.matmul(h_bank(n), w1_hi[:, e, cols], x_hi[m][:, :], start=True, stop=False)
                pe.matmul(h_bank(n), w1_hi[:, e, cols], x_lo[m][:, :], start=False, stop=False)
                pe.matmul(h_bank(n), w1_lo[:, e, cols], x_hi[m][:, :], start=False, stop=True)\
                  .then_inc(hidden_ready, 1)

        def expert_out(it, e):
            need(pe, hT_ready, at(it, HID, FC * (e + 1)))
            need(pe, y_added, at(it, E, e - YRING + 1))
            for q in range(QT):
                for c in range(FC):
                    last = pe.matmul(y_bank(e)[:, q * C:(q + 1) * C], hT[:, e % HTRING, c, q * P:(q + 1) * P],
                                     w2[:, e, c, :], start=(c == 0), stop=(c == FC - 1))
            last.then_inc(y_ready, 1)

        first = (None, 0)

        def prepare(s):
            if s == 11:
                turn_xn(first)
            if s == 13:
                pe.wait_ge(gate_in, 48)
                gate(first)

        def batch(it, i):
            nxt = later(it, 1)
            need(pe, x_lo_ready, at(it, 1, 1))
            for e in range(E):
                hidden(it, e)
                if i == 0:
                    tail_of[0](e)
                if e >= 1:
                    expert_out(it, e - 1)
                elif i >= 1:
                    expert_out(later(it, -1), E - 1)
                if i + 1 < B:
                    if e == 4:
                        turn_xn(nxt)
                    if e == 5:
                        gate(nxt)

        def run(tail):
            tail_of.append(tail)
            pe.wait_ge(shared["w1_split"], 2)
            schedule(pe, batch)
            expert_out((None, B - 1), E - 1)

        tail_of = []
        return prepare, run

    return experts_sync, experts_gpsimd, experts_tensor, experts_scalar, experts_vector


def layer(nc, d, out):
    with ExitStack() as ctx:
        def sb(name, shape, dt=F32):
            return ctx.enter_context(nc.sbuf_tensor(name, shape, dt))

        X1 = sb("X1", [P, B * QT, C])
        shared = {
            "ident": sb("ident", [P, P]),
            "x_in": sb("x_in", [P, QT, C]),
            "qk_full": [sb("q_full", [P, S]), sb("k_full", [P, S])],
            "xn": sb("xn", [P, QT, C]),
            "xnT": sb("xnT", [P, S]),
            "qk_hi": [sb("q_hi", [P, S], F32R), sb("k_hi", [P, S], F32R)],
            "qk_lo": [sb("q_lo", [P, S], F32R), sb("k_lo", [P, S], F32R)],
            "probs": sb("probs", [P, PRING, J, S]),
            "w2": sb("w2", [P, E, FC, C]),
            "b1": sb("b1", [P, E * FC]),
            "PS": ctx.enter_context(nc.psum_tensor("PS", [P, 8, S], F32)),
            "experts_in": ctx.enter_context(nc.semaphore("experts_in")),
            "w1_split": ctx.enter_context(nc.semaphore("w1_split")),
            "ident_ready": ctx.enter_context(nc.semaphore("ident_ready")),
        }
        room = sb("room", [P, J, G, S], F32R)
        shared["room"] = room
        parts = room[:, :, :, :].rearrange("p j g (k n) -> p j (g k) n", n=F)
        shared["w1_hi"], shared["w1_lo"] = parts[:, 0], parts[:, 1]
        att_sync, att_gpsimd, att_tensor, att_scalar, att_vector = attention(nc, ctx, d, X1, shared)
        exp_sync, exp_gpsimd, exp_tensor, exp_scalar, exp_vector = experts(nc, ctx, d, X1, shared, out)
        block = ctx.enter_context(nc.Block())

        @block.sync
        def _(sp):
            att_sync(sp)
            exp_sync(sp)

        @block.gpsimd
        def _(pool):
            att_gpsimd(pool)
            exp_gpsimd(pool)

        @block.tensor
        def _(pe):
            prepare, run = exp_tensor(pe)
            run(att_tensor(pe, prepare))

        @block.scalar
        def _(act):
            prepare, run = exp_scalar(act)
            run(att_scalar(act, prepare))

        @block.vector
        def _(dve):
            prepare, run = exp_vector(dve)
            run(att_vector(dve, prepare))


def _constants():
    import numpy as np

    slopes = 0.5 ** np.arange(H, dtype=np.float32).reshape(G, J).T
    pos = np.arange(S, dtype=np.float32)
    rise = slopes[:, :, None] * pos
    own = np.eye(J, dtype=np.float32)[:, :, None, None]
    q_aug = np.concatenate([np.ones((J, G, S)), -rise])
    k_aug = np.concatenate([own * rise, own * np.ones((J, G, S)),
                            own * np.ones((J, G, S)), own * np.ones((J, G, S))])
    return {"ident": np.eye(P, dtype=np.float32), "q_aug": q_aug.astype(np.float32),
            "k_aug": k_aug.astype(np.float32)}


def kernel(**inputs):
    import numpy as np
    import concourse.bacc as bacc
    from concourse.bass_utils import run_bass_kernel_spmd

    given = {k: np.asarray(v) for k, v in inputs.items()}
    att = lambda n: given["L0_attn_" + n]
    ffn = lambda n: given["L0_ffn_" + n]
    order = np.arange(C).reshape(2, GH, J, D).transpose(0, 2, 3, 1).reshape(C)
    pick = {"q": order, "k": order, "v": np.arange(C), "o": np.arange(C)}
    taken = {n: np.arange(C) for n in "qkv"}
    taken["o"] = np.arange(C).reshape(PAIRS, 2, J, D).transpose(0, 2, 1, 3).reshape(C)
    arrays = {"x": att("x"), "rezero": att("rezero").reshape(1, 1)}
    arrays["WT"] = np.stack([att("W" + n).T[taken[n]][:, pick[n]] for n in "qkvo"])
    arrays["A"] = np.stack([att("A" + n)[:, taken[n]] for n in "qkvo"])
    arrays["BT"] = np.stack([att("B" + n).T[:, pick[n]] for n in "qkvo"])
    arrays["qk_bias"] = np.stack([att("bq")[order], att("bk")[order]], axis=1)
    arrays["bv"] = att("bv").reshape(1, C)
    arrays["bo"] = att("bo").reshape(1, C)
    arrays["gate_w"] = ffn("gate_w")
    arrays["gate_b"] = ffn("gate_b").reshape(1, E)
    arrays["w1"] = ffn("w1")
    arrays["b1T"] = ffn("b1").reshape(E * FC, P).T
    arrays["w2"] = ffn("w2")
    arrays["b2"] = ffn("b2").reshape(1, E * C)
    arrays.update(_constants())

    nc = bacc.Bacc("TRN2", target_bir_lowering=False, num_devices=1)
    d, sent = {}, {}
    for name, a in arrays.items():
        sent["in_" + name] = np.ascontiguousarray(a)
        d[name] = nc.dram_tensor("in_" + name, a.shape, mybir.dt.from_np(a.dtype), kind="ExternalInput").ap()
    out = nc.dram_tensor("out", (B, S, C), F32, kind="ExternalOutput").ap()
    layer(nc, d, out)
    r = run_bass_kernel_spmd(nc, [sent], core_ids=[0])
    return r.results[0]["out"]
```
